# Optimizing a Trainium2 kernel written in Bass

```python
import numpy as np
import jax
import jax.numpy as jnp

def _softmax(x, axis=-1):
    return jax.nn.softmax(x, axis=axis)

def _gelu(x):
    return jax.nn.gelu(x, approximate=True)

def _silu(x):
    return jax.nn.silu(x)

def _sigmoid(x):
    return jax.nn.sigmoid(x)

def _layernorm(x, axis=-1, eps=1e-05):
    m = jnp.mean(x, axis=axis, keepdims=True)
    v = jnp.var(x, axis=axis, keepdims=True)
    return (x - m) / jnp.sqrt(v + eps)

def _scatter_add(tgt, idx, src, axis=0):
    return tgt.at[idx].add(src)

def _segment_sum(src, seg, n):
    return jax.ops.segment_sum(src, seg, n)
kernel_name = 'mk_vit_tower_d1_tok_img1024_r4_f36d66'

def setup_inputs(seed: int=0):
    np.random.seed(seed)
    _w = jnp.asarray

    def _rec_inputs():
        import jax
        import jax.numpy as jnp
        _rk = jax.random.key(seed)
        x = -0.000356955 + 1 * jax.random.normal(jax.random.fold_in(_rk, 1), (64, 3, 224, 224), jnp.float32)
        return x
    x = _rec_inputs()

    def _L0_tok_setup():
        import jax, jax.numpy as jnp
        import numpy as np
        PH, PW = (16, 16)
        key = jax.random.key(seed)
        k1, k2 = jax.random.split(key)
        B, C, H, W_ = (128, 3, 224, 224)
        embed_dim = 256
        patch_dim = C * PH * PW
        x = jax.random.normal(k1, (B, C, H, W_), dtype=jnp.float32)
        W = jax.random.normal(k2, (embed_dim, patch_dim), dtype=jnp.float32) * 0.02
        b = jnp.zeros((embed_dim,), dtype=jnp.float32)
        return {'x': x, 'W': W, 'b': b}
    _L0_tok_all = _L0_tok_setup()
    _L0_tok_in = {k: v for k, v in _L0_tok_all.items() if k in ('W', 'b')}
    del _L0_tok_all

    def _L0_attn_setup():
        import jax, jax.numpy as jnp
        import numpy as np
        HEADS = 8
        KS = 4
        ST = 2
        key = jax.random.key(seed)
        k1, k2, k3, k4 = jax.random.split(key, 4)
        B, L, C = (8, 512, 256)
        s = C ** (-0.5)
        x = jax.random.normal(k1, (B, L, C), dtype=jnp.float32)
        w_qkv = jax.random.normal(k2, (C, 3 * C), dtype=jnp.float32) * s
        w_out = jax.random.normal(k3, (C, C), dtype=jnp.float32) * s
        b_out = jax.random.normal(k4, (C,), dtype=jnp.float32)
        return {'x': x, 'w_qkv': w_qkv, 'w_out': w_out, 'b_out': b_out}
    _L0_attn_all = _L0_attn_setup()
    _L0_attn_in = {k: v for k, v in _L0_attn_all.items() if k in ('w_qkv', 'w_out', 'b_out')}
    del _L0_attn_all

    def _L0_ffn_setup():
        import jax, jax.numpy as jnp
        import numpy as np
        TOPK = 2
        CAPACITY_FACTOR = 1.0
        EPS = 1e-06
        B, S, D = (4, 1024, 256)
        E = 8
        SUB_H = 512 // E
        key = jax.random.key(seed)
        ks = jax.random.split(key, 7)
        x = jax.random.normal(ks[0], (B, S, D), dtype=jnp.float32)
        w_gate_w = jax.random.normal(ks[1], (D, E), dtype=jnp.float32) * 0.02
        w_gate_b = jnp.zeros((E,), jnp.float32)
        W1 = jax.random.normal(ks[2], (E, D, SUB_H), dtype=jnp.float32) * 0.02
        b1 = jnp.zeros((E, SUB_H), jnp.float32)
        W2 = jax.random.normal(ks[3], (E, SUB_H, D), dtype=jnp.float32) * 0.02
        b2 = jnp.zeros((E, D), jnp.float32)
        return {'x': x, 'w_gate_w': w_gate_w, 'w_gate_b': w_gate_b, 'W1': W1, 'b1': b1, 'W2': W2, 'b2': b2}
    _L0_ffn_all = _L0_ffn_setup()
    _L0_ffn_in = {k: v for k, v in _L0_ffn_all.items() if k in ('w_gate_w', 'w_gate_b', 'W1', 'b1', 'W2', 'b2')}
    del _L0_ffn_all
    return {'x': x, 'L0_tok_W': _L0_tok_in['W'], 'L0_tok_b': _L0_tok_in['b'], 'L0_attn_w_qkv': _L0_attn_in['w_qkv'], 'L0_attn_w_out': _L0_attn_in['w_out'], 'L0_attn_b_out': _L0_attn_in['b_out'], 'L0_ffn_w_gate_w': _L0_ffn_in['w_gate_w'], 'L0_ffn_w_gate_b': _L0_ffn_in['w_gate_b'], 'L0_ffn_W1': _L0_ffn_in['W1'], 'L0_ffn_b1': _L0_ffn_in['b1'], 'L0_ffn_W2': _L0_ffn_in['W2'], 'L0_ffn_b2': _L0_ffn_in['b2']}

def reference(x, L0_tok_W, L0_tok_b, L0_attn_w_qkv, L0_attn_w_out, L0_attn_b_out, L0_ffn_w_gate_w, L0_ffn_w_gate_b, L0_ffn_W1, L0_ffn_b1, L0_ffn_W2, L0_ffn_b2):
    import jax
    import jax.numpy as jnp

    def _L0_tok_ref(x, W, b):
        import jax, jax.numpy as jnp
        import numpy as np
        PH, PW = (16, 16)
        B, C, H, Wd = x.shape
        nh, nw = (H // PH, Wd // PW)
        p = x.reshape(B, C, nh, PH, nw, PW).transpose(0, 2, 4, 1, 3, 5)
        p = p.reshape(B, nh * nw, C * PH * PW)
        return jnp.einsum('bnp,dp->bnd', p, W) + b

    def _L0_attn_ref(x, w_qkv, w_out, b_out):
        import jax, jax.numpy as jnp
        import numpy as np
        HEADS = 8
        KS = 4
        ST = 2
        B, L, C = x.shape
        H = HEADS
        Dh = C // H
        scale = C ** (-0.5)
        qkv = x @ w_qkv
        starts = jnp.arange(0, L - KS + 1, ST)
        idx = starts[:, None] + jnp.arange(KS)[None, :]
        win = qkv[:, idx]
        q, k, v = jnp.split(win, 3, axis=-1)
        N = starts.shape[0]
        q = q.reshape(B, N, KS, H, Dh)
        k = k.reshape(B, N, KS, H, Dh)
        v = v.reshape(B, N, KS, H, Dh)
        dots = jnp.einsum('bnqhd,bnkhd->bnhqk', q, k) * scale
        attn = jax.nn.softmax(dots, axis=-1)
        o = jnp.einsum('bnhqk,bnkhd->bnqhd', attn, v)
        o = o.reshape(B, N, KS, C)
        y = o @ w_out + b_out
        out = jnp.zeros((B, L, C), dtype=x.dtype)
        out = out.at[:, idx.reshape(-1), :].add(y.reshape(B, N * KS, C))
        return out

    def _L0_ffn_ref(x, w_gate_w, w_gate_b, W1, b1, W2, b2):
        import jax, jax.numpy as jnp
        import numpy as np
        TOPK = 2
        CAPACITY_FACTOR = 1.0
        EPS = 1e-06
        B, S, D = (4, 1024, 256)
        E = 8
        SUB_H = 512 // E
        Bx, Sx, Dx = x.shape
        Ex = w_gate_b.shape[0]
        K = Sx // 2
        capacity = int(CAPACITY_FACTOR * Bx)
        gate_scores = jax.nn.softmax(x @ w_gate_w + w_gate_b, axis=-1)
        _, top_idx = jax.lax.top_k(gate_scores, TOPK)
        mask = jax.nn.one_hot(top_idx, Ex, dtype=gate_scores.dtype).sum(axis=-2)
        masked = gate_scores * mask
        denom = masked.sum(axis=0, keepdims=True) + EPS
        route = masked / denom * capacity
        route_eb = jnp.transpose(route, (2, 0, 1))
        _, seq_ids = jax.lax.top_k(route_eb, K)
        seq_ids = jnp.sort(seq_ids, axis=-1)
        xg = jax.vmap(lambda idx: jnp.take_along_axis(x, idx[..., None], axis=1))(seq_ids)
        h = jnp.einsum('ebkd,edh->ebkh', xg, W1) + b1[:, None, None, :]
        h = jax.nn.gelu(h, approximate=False)
        o = jnp.einsum('ebkh,ehd->ebkd', h, W2) + b2[:, None, None, :]
        flat_ids = (jnp.arange(Bx)[None, :, None] * Sx + seq_ids).reshape(-1)
        outs = jnp.zeros((Bx * Sx, Dx), x.dtype).at[flat_ids].add(o.reshape(-1, Dx))
        return outs.reshape(Bx, Sx, Dx)
    h = _L0_tok_ref(x, L0_tok_W, L0_tok_b)
    h = h + _L0_attn_ref(_layernorm(h, axis=-1), L0_attn_w_qkv, L0_attn_w_out, L0_attn_b_out)
    h = h + _L0_ffn_ref(_layernorm(h, axis=-1), L0_ffn_w_gate_w, L0_ffn_w_gate_b, L0_ffn_W1, L0_ffn_b1, L0_ffn_W2, L0_ffn_b2)
    return h

_drawn_inputs = setup_inputs


def setup_inputs(seed=0):
    import zlib

    import numpy as np

    out = dict(_drawn_inputs(seed))
    spreads = {'L0_tok_b': (0.0, 0.1),
     'L0_ffn_w_gate_b': (0.0, 0.1),
     'L0_ffn_b1': (0.0, 0.8),
     'L0_ffn_b2': (0.0, 0.1)}
    factors = {}
    for name, (base, spread) in spreads.items():
        noise = np.random.default_rng([zlib.crc32(name.encode()), seed]).standard_normal(out[name].shape)
        drawn = base * np.exp(spread * noise) if base else spread * noise
        out[name] = jnp.asarray(drawn.astype(out[name].dtype))
    for name, factor in factors.items():
        out[name] = (out[name] * factor).astype(out[name].dtype)
    return out
```

```python
from contextlib import ExitStack

import concourse.bass as bass
from concourse import mybir

F32 = mybir.dt.float32
F32R = mybir.dt.float32r
BF16 = mybir.dt.bfloat16
ALU = mybir.AluOpType
ACT = mybir.ActivationFunctionType
AX = mybir.AxisListType

C = 256
MC = C // 128
PATCH = 16
SIDE = 14
SEQ = SIDE * SIDE
IMG = 4
ROWS = IMG * SIDE
TOK = IMG * SEQ
HEADS, DH, KS, STRIDE = 8, 32, 4, 2
HALO = STRIDE
POS = 32
Q = POS - 2 * HALO
BLOCKS = TOK // Q
TILES = BLOCKS // 4
GPOS = BLOCKS * POS
HALF = GPOS // 2
BAND = 36
HQ = 4
IDX = HQ * TILES * MC
E, SUB, TOPK = 8, 64, 2
HID = E * SUB // 128
KC = 3 * PATCH * PATCH // 128
LN_EPS = 1e-5
GATE_EPS = 1e-6
SCALE = float(C) ** -0.5
PICK = SEQ // 2
PAD = -PICK % 8
BIG = 1e30


def shape_constants(np):
    pos = np.arange(128)
    i = pos % POS
    pair = i // 2
    kap = np.arange(BAND)
    band = ((np.abs(kap[None, :] // 2 - pair[:, None]) <= 1) & (kap[None, :] < POS)).astype(np.float32)
    slot = (np.arange(6) // 2)[None, :]
    out0 = (pair[:, None] + 1) % 3 == slot
    out1 = (pair[:, None] - 1) % 3 == slot
    window = np.stack([np.where(out0, -BIG, 0), np.where(out1, -BIG, 0)], 1).astype(np.float32)
    block = (np.arange(TILES)[None, :] * 4 + (pos // POS)[:, None]) % (SEQ // Q)
    has0 = ~((block == 0) & (pair[:, None] == 1))
    has1 = ~((block == SEQ // Q - 1) & (pair[:, None] == POS // 2 - 2))
    has = np.stack([has0, has1], 1).astype(np.float32)
    there = np.broadcast_to(has[:, :, None, :, None], (128, 2, HQ, TILES, MC)).reshape(128, 2 * IDX)
    windows = has.sum(1).T.reshape(1, TILES * 128)
    e = np.arange(E)
    lower = np.broadcast_to((e[None, :] < e[:, None]).reshape(1, E * E), (128, E * E))
    same = (pos[:, None] % E == pos[None, :] % E)
    spread = np.zeros((E, HID * 128), np.float32)
    for c in range(HID):
        for m in range(128):
            spread[(c * 128 + m) // SUB, c * 128 + m] = 1
    f = lambda a: np.ascontiguousarray(a, dtype=np.float32)
    return {"c_ident": f(np.eye(128)), "c_band": f(band), "c_window": f(window.reshape(128, 12)),
            "c_there": f(there), "c_windows": f(windows), "c_lower": f(lower), "c_same": f(same),
            "c_spread": f(spread)}


class Steps:

    def __init__(self, eng, sem, per_group):
        self.eng, self.sem, self.per_group = eng, sem, per_group

    def group(self, g):
        self.base, self.n = g * self.per_group, 0

    def did(self, ins):
        ins.then_inc(self.sem, 1)
        self.n += 1

    def wait(self):
        self.eng.wait_ge(self.sem, self.base + self.n)

    def end(self):
        assert self.n == self.per_group, self.n


def vit_layer(nc, x, w_patch, b_patch, w_qkv, w_out, b_out, w_gate, b_gate, w1, b1, w2, b2,
              c_ident, c_band, c_window, c_there, c_windows, c_lower, c_same, c_spread, out):
    B = x.shape[0]
    G = B // IMG
    NTOK = B * SEQ
    CH = B * E // 128
    CIMG = 128 // E

    h2n_d = nc.dram_tensor("normalised_tokens", (G, 128, TILES * C), F32, kind="Internal").ap()
    score_d = nc.dram_tensor("gate_scores", (E, NTOK), F32, kind="Internal").ap()
    mask_d = nc.dram_tensor("picked", (E, NTOK), BF16, kind="Internal").ap()

    def view(ap, *dims):
        return bass.AP(ap.tensor, ap.offset, [list(ap.ap[0])] + [list(d) for d in dims])

    weights = ExitStack()
    with weights:
        def tensor(stack, name, shape, dt=F32):
            return stack.enter_context(nc.sbuf_tensor(name, shape, dt))

        def sem(name):
            return weights.enter_context(nc.semaphore(name))

        bank = [weights.enter_context(nc.psum_tensor(f"bank{n}", [128, 512], F32)) for n in range(8)]
        att, dense = bank[:4], bank[4:]

        ident = tensor(weights, "ident", [128, 128])
        same = tensor(weights, "same", [128, 128])
        b1s = tensor(weights, "b1s", [128, HID])
        b2s = tensor(weights, "b2s", [E, C])
        spread32 = tensor(weights, "spread32", [E, HID * 128])
        spread = tensor(weights, "spread", [E, HID * 128], BF16)

        one = ExitStack()
        band = tensor(one, "band", [128, BAND])
        window = tensor(one, "window", [128, 12])
        there = tensor(one, "there", [128, 2 * IDX])
        windows = tensor(one, "windows", [1, GPOS])
        lower = tensor(one, "lower", [128, E * E])
        bps = tensor(one, "bps", [128, MC])
        bouts = tensor(one, "bouts", [1, C])
        wgs = tensor(one, "wgs", [128, MC, E])
        bgs = tensor(one, "bgs", [1, E])
        ones = tensor(one, "ones", [1, 128])
        eps = tensor(one, "eps", [128, 2 * TILES])
        wp_h = tensor(one, "wp_h", [128, KC * C], F32R)
        wp_l = tensor(one, "wp_l", [128, KC * C], F32R)
        wqkv_h = tensor(one, "wqkv_h", [128, MC * 3 * C], F32R)
        wqkv_l = tensor(one, "wqkv_l", [128, MC * 3 * C], F32R)
        wo_h = tensor(one, "wo_h", [128, MC * C], F32R)
        wo_l = tensor(one, "wo_l", [128, MC * C], F32R)
        raw = tensor(one, "raw", [2 * ROWS, 8 * SIDE * PATCH])
        patches = tensor(one, "patches", [2 * ROWS, 3, SIDE, 128])
        xT_h = tensor(one, "xT_h", [128, KC, HALO + TOK + HALO], F32R)
        xT_l = tensor(one, "xT_l", [128, KC, HALO + TOK + HALO], F32R)
        hT = tensor(one, "hT", [128, MC, GPOS])
        hpos = tensor(one, "hpos", [128, TILES, C])
        hres = tensor(one, "hres", [128, TILES, C])
        hn = tensor(one, "hn", [128, TILES, C])
        hnT_h = tensor(one, "hnT_h", [128, MC, GPOS], F32R)
        hnT_l = tensor(one, "hnT_l", [128, MC, GPOS], F32R)
        qT = tensor(one, "qT", [128, MC, GPOS])
        kT = tensor(one, "kT", [128, MC, GPOS])
        v = tensor(one, "v", [128, TILES, C])
        banded = tensor(one, "banded", [128, IDX, BAND])
        six = tensor(one, "six", [128, IDX, 6])
        win = tensor(one, "win", [128, 2, IDX, 6])
        wstat = tensor(one, "wstat", [128, 2 * IDX])
        prob = tensor(one, "prob", [128, IDX, 6])
        oT_h = tensor(one, "oT_h", [128, TILES, MC, 128], F32R)
        oT_l = tensor(one, "oT_l", [128, TILES, MC, 128], F32R)
        h2 = tensor(one, "h2", [128, TILES, C])
        hn2 = kT[:, :, :].rearrange("p m n -> p (m n)").rearrange("p (t c) -> p t c", c=C)
        hn2T = hT
        stat = [tensor(one, f"stat{n}", [128, TILES, 6]) for n in range(2)]
        mv = [tensor(one, f"mv{n}", [128, TILES, 2]) for n in range(2)]
        vare = [tensor(one, f"vare{n}", [128, TILES]) for n in range(2)]
        rstd = [tensor(one, f"rstd{n}", [128, TILES]) for n in range(2)]
        shift = [tensor(one, f"shift{n}", [128, TILES]) for n in range(2)]
        gate = tensor(one, "gate", [128, TILES, E])
        gstat = tensor(one, "gstat", [128, 2 * TILES])
        above = view(win[:, 0, 0, 0:1], [E * E, TILES], [E, E], [1, E])
        level = tensor(one, "level", [128, TILES, E, E])
        rank = tensor(one, "rank", [128, TILES, E])
        masked = tensor(one, "masked", [128, 64])
        scoresT = tensor(one, "scoresT", [128, 64])
        pT = qT[:, :, :].rearrange("p m n -> p (m n)").rearrange("p (k j) -> p k j", j=POS)
        one.close()

        route = tensor(weights, "route", [128, CH, SEQ + PAD])
        rden = tensor(weights, "rden", [128, SEQ])
        best = tensor(weights, "best", [128, CH, 8])
        picked = tensor(weights, "picked_sb", [128, CH, SEQ], BF16)

        three = ExitStack()
        w1s = tensor(three, "w1s", [128, MC * E * SUB])
        w2s = tensor(three, "w2s", [128, HID * C])
        w1_h = tensor(three, "w1_h", [128, MC * E * SUB], F32R)
        w1_l = tensor(three, "w1_l", [128, MC * E * SUB], F32R)
        w2_h = tensor(three, "w2_h", [128, HID * C], F32R)
        w2_l = tensor(three, "w2_l", [128, HID * C], F32R)
        t_in = tensor(three, "t_in", [128, MC, GPOS])
        t_h = tensor(three, "t_h", [128, MC, GPOS], F32R)
        t_l = tensor(three, "t_l", [128, MC, GPOS], F32R)
        h_in = tensor(three, "h_in", [4 * Q, TILES, C])
        y_out = tensor(three, "y_out", [4 * Q, TILES, C])
        mask16 = tensor(three, "mask16", [E, TOK], BF16)
        mask32 = tensor(three, "mask32", [E, TOK])
        hid = tensor(three, "hid", [128, HID, TOK])
        hid_h = tensor(three, "hid_h", [128, HID, TOK], F32R)
        hid_l = tensor(three, "hid_l", [128, HID, TOK], F32R)
        three.close()

        FILLS = {"first": [("T", 12), ("E", 4), ("F", 4), ("N", 4)],
                 "loop": [("Q", 8), ("V", 4), ("T", 12), ("E", 4), ("F", 4), ("O", 4), ("N", 4), ("L", 4)],
                 "last": [("Q", 8), ("V", 4), ("O", 4), ("L", 4)]}
        FIRST_TURNS = sum(n for _, n in FILLS["first"]) // 4
        LOOP_TURNS = sum(n for _, n in FILLS["loop"]) // 4

        def fill(part, stage, n, g):
            at = n
            for name, count in FILLS[part]:
                if name == stage:
                    break
                at += count
            turns = at // 4
            if part != "first":
                turns = g * LOOP_TURNS + (FIRST_TURNS + turns)
            return at % 4, turns

        def wait_read(eng, part, stage, n, g):
            b, turns = fill(part, stage, n, g)
            eng.wait_ge(dense_free[b], turns + 1)

        PAIRS = [(0, 1), (2, 3), (4, 5), (6,)]
        TSTEPS = [(c, w, min(4, SIDE - w)) for c in range(3) for w in range(0, SIDE, 4)]
        assert len(TSTEPS) == 12 and len(PAIRS) == 4

        dense_full = [sem(f"dense_full{b}") for b in range(4)]
        dense_free = [sem(f"dense_free{b}") for b in range(4)]
        consts_in = sem("consts_in")
        weights_in = sem("weights_in")
        weights_split = sem("weights_split")
        setup = sem("setup")
        raw_loaded, patched = sem("raw_loaded"), sem("patched")
        xT_hi = sem("xT_hi")
        hres_copied = sem("hres_copied")
        var_ready = [sem(f"var_ready{n}") for n in range(2)]
        rstd_ready = [sem(f"rstd_ready{n}") for n in range(2)]
        hn_ready = sem("hn_ready")
        hnT_hi = sem("hnT_hi")
        scores_ready = sem("scores_ready")
        shifted, exped = sem("shifted"), sem("exped")
        spread_done, pT_ready = sem("spread_done"), sem("pT_ready")
        attended = sem("attended")
        oT_hi, oT_lo = sem("oT_hi"), sem("oT_lo")
        h2_stored = sem("h2_stored")
        hn2_ready = sem("hn2_ready")
        hn2T_stored = sem("hn2T_stored")
        gates_done = sem("gates_done")
        gshifted, gexped = sem("gshifted"), sem("gexped")
        scoresT_ready, scoresT_stored = sem("scoresT_ready"), sem("scoresT_stored")
        ln_step = [sem(f"ln_step{n}") for n in range(2)]
        soft_step, gate_step = sem("soft_step"), sem("gate_step")

        passed = sem("passed")

        def settle(eng):
            eng.sem_inc(passed, 1)

        def patch_views(d, xt, c, w0, nw):
            src = d[:, 0:nw * 2 * ROWS].rearrange("k (w f r) -> k f r w", f=2, r=ROWS)
            dst = xt[:, 2 * c:2 * c + 2, HALO:HALO + TOK].rearrange("k f (r w) -> k f r w", w=SIDE)[:, :, :, w0:w0 + nw]
            return src, dst

        def channel_views(d, a, tiles):
            src = d[:, 0:256 * len(tiles)].rearrange("p (t m c) -> p m t c", m=MC, c=128)
            dst = a[:, :, tiles[0] * 128:(tiles[-1] + 1) * 128].rearrange("p m (t c) -> p m t c", c=128)
            return src, dst

        x_v = x.rearrange("(g b) c (n f r) w -> g f c b n (r w)", b=IMG, n=SIDE, f=2)
        out_v = out.rearrange("(g t b i) n -> g b i t n", t=TILES, b=4, i=Q)

        with nc.Block() as block:
            @block.sync
            def _(sp):
                for dst, src in ((ident, c_ident), (band, c_band), (window, c_window), (there, c_there),
                                 (windows, c_windows), (lower, c_lower), (bps, b_patch), (bouts, b_out),
                                 (wgs, w_gate), (bgs, b_gate), (same, c_same)):
                    d = dst[:, :, :].rearrange("p m e -> p (m e)") if dst is wgs else dst[:, :]
                    sp.dma_start(d, src).then_inc(consts_in, 16)

                def load(p):
                    for c in range(3):
                        sp.wait_ge(patched, p * 3 + c)
                        for f in range(2):
                            for b in range(IMG):
                                r = f * ROWS + b * SIDE
                                sp.dma_start(raw[r:r + SIDE, :], x_v[p, f, c, b]).then_inc(raw_loaded, 16)

                def weight_loads():
                    sp.dma_start(view(hpos[:, 0, 0:1], [1, KC * C]), w_patch).then_inc(weights_in, 16)
                    sp.dma_start(view(hT[:, 0, 0:1], [1, MC * 3 * C]), w_qkv).then_inc(weights_in, 16)
                    sp.dma_start(view(hn[:, 0, 0:1], [1, MC * C]), w_out).then_inc(weights_in, 16)

                def store(part, g):
                    wait_read(sp, part, "O", 3, g)
                    for b in range(4):
                        sp.dma_start(out_v[g, b], h2[b * POS + HALO:b * POS + HALO + Q, :, :]).then_inc(h2_stored, 16)
                    wait_read(sp, part, "L", 3, g)
                    sp.dma_start(h2n_d[g], view(hn2T[:, 0, 0:1], [1, MC * GPOS])).then_inc(hn2T_stored, 16)
                    sp.wait_ge(scoresT_ready, g + 1)
                    for b in range(4):
                        for half in range(2):
                            tiles = min(4, TILES - 4 * half)
                            at = g * TOK + half * 16 * Q + b * Q
                            dst = bass.AP(score_d.tensor, score_d.offset + at, [[4 * Q, tiles], [NTOK, E], [1, Q]])
                            src = scoresT[b * 32:b * 32 + tiles * E, half * 32 + HALO:half * 32 + HALO + Q]
                            sp.dma_start(dst, src).then_inc(scoresT_stored, 16)

                for stored in (h2_stored, hn2T_stored, scoresT_stored):
                    sp.sem_inc(stored, 1)
                weight_loads()
                load(0)
                load(1)
                with sp.Fori(0, G - 2) as g:
                    load(g + 2)
                    store("loop", g)
                store("loop", G - 2)
                store("last", G - 1)
                sp.wait_ge(h2_stored, G * 64 + 1)
                sp.wait_ge(hn2T_stored, G * 16 + 1)
                sp.wait_ge(scoresT_stored, G * 128 + 1)

            @block.gpsimd
            def _(pool):
                pool.memset(ones[:, :], 1.0)
                pool.memset(eps[:, :], -0.5)
                pool.memset(masked[:, :], 0.0)
                pool.memset(banded[:, :, POS:BAND], 0.0).then_inc(setup, 1)
                for xt in (xT_h, xT_l):
                    for edge in (0, HALO + TOK):
                        last = pool.memset(xt[:, :, edge:edge + HALO].bitcast(F32), 0.0)
                last.then_inc(setup, 1)
                pool.wait_ge(setup, 2)

                def root(n, g):
                    pool.wait_ge(var_ready[n], g + 1)
                    pool.tensor_tensor(rstd[n][:, :], vare[n][:, :], eps[:, 0:TILES], ALU.pow).then_inc(rstd_ready[n], 1)

                def copy_residual(part, at):
                    wait_read(pool, part, "F", 3, at)
                    if part != "first":
                        wait_read(pool, part, "O", 3, at)
                    settle(pool)
                    pool.tensor_copy(view(hres[:, 0, 0:1], [1, TILES * C]),
                                     view(hpos[:, 0, 0:1], [1, TILES * C])).then_inc(hres_copied, 1)

                def gather_patches(p, part, at):
                    for c in range(3):
                        pool.wait_ge(raw_loaded, p * 384 + 128 * (c + 1))
                        if part is not None:
                            b, turns = fill(part, "T", 4 * c + 3, at)
                            pool.wait_ge(dense_full[b], turns + 1)
                        settle(pool)
                        pool.tensor_scalar(patches[:, c, :, :].rearrange("p w (r i) -> p r w i", i=PATCH),
                                           raw[:, :].rearrange("p (r w i) -> p r w i", r=8, i=PATCH),
                                           1.0, 0.0, ALU.mult, ALU.add).then_inc(patched, 1)

                gather_patches(0, None, 0)
                gather_patches(1, "first", 0)
                root(0, 0)
                copy_residual("first", 0)
                with pool.Fori(0, G - 2) as g:
                    gather_patches(g + 2, "loop", g)
                    root(0, g + 1)
                    copy_residual("loop", g)
                    root(1, g)
                root(0, G - 1)
                copy_residual("loop", G - 2)
                root(1, G - 2)
                root(1, G - 1)

            @block.tensor
            def _(pe):
                def begin(part, stage, n, g):
                    b, turns = fill(part, stage, n, g)
                    if not isinstance(turns, int) or turns > 0:
                        pe.wait_ge(dense_free[b], turns)
                    return b, dense[b]

                def product(o, a_h, a_l, b_h, b_l, start, stop):
                    pe.matmul(o, a_h, b_h, start=start, stop=False)
                    pe.matmul(o, a_l, b_h, start=False, stop=False)
                    return pe.matmul(o, a_h, b_l, start=False, stop=stop)

                def transpose_patches(part, p):
                    for n, (c, w0, nw) in enumerate(TSTEPS):
                        if w0 == 0:
                            pe.wait_ge(patched, p * 3 + c + 1)
                        b, d = begin(part, "T", n, p if part == "first" else p - 1)
                        for w in range(nw):
                            mm = pe.transpose(d[:, w * 2 * ROWS:(w + 1) * 2 * ROWS], patches[:, c, w0 + w, :], ident[0:2 * ROWS, 0:2 * ROWS])
                        mm.then_inc(dense_full[b], 1)

                def embed(part, p):
                    wait_read(pe, part, "T", 11, p if part == "first" else p - 1)
                    for n in range(4):
                        u, m = divmod(n, MC)
                        b, d = begin(part, "E", n, p if part == "first" else p - 1)
                        for k in range(KC):
                            wh, wl = (w[:, k * C + m * 128:k * C + m * 128 + 128] for w in (wp_h, wp_l))
                            xh, xl = (view(xt[:, k, u * (TOK // 2):u * (TOK // 2) + 1], [Q, BLOCKS // 2], [1, POS])
                                      for xt in (xT_h, xT_l))
                            mm = product(d[:, 0:HALF], wh, wl, xh, xl, k == 0, k == KC - 1)
                        mm.then_inc(dense_full[b], 1)

                def turn(part, stage, g, wait, src):
                    for n, tiles in enumerate(PAIRS):
                        wait(n)
                        b, d = begin(part, stage, n, g)
                        for t in tiles:
                            for m in range(MC):
                                at = (t % 2) * 256 + m * 128
                                mm = pe.transpose(d[:, at:at + 128], src(t, m), ident[:, :])
                        mm.then_inc(dense_full[b], 1)

                def h_to_positions(part, p, at):
                    turn(part, "F", at, lambda n: wait_read(pe, part, "E", 1 if n == 0 else 3, at),
                         lambda t, m: hT[:, m, t * 128:t * 128 + 128])

                def hn_to_channels(part, p, at):
                    turn(part, "N", at, lambda n: pe.wait_ge(hn_ready, p * 4 + n + 1),
                         lambda t, m: hn[:, t, m * 128:m * 128 + 128])

                def hn2_to_channels(part, g):
                    turn(part, "L", g, lambda n: pe.wait_ge(hn2_ready, g * 4 + n + 1),
                         lambda t, m: hn2[:, t, m * 128:m * 128 + 128])

                def qkv(part, g):
                    b, turns = fill(part, "Q", 3, g)
                    pe.wait_ge(dense_free[b], turns)
                    for n in range(8):
                        mo, u = divmod(n, 2)
                        b, d = begin(part, "Q", n, g)
                        for k in range(MC):
                            at = k * 3 * C + mo * 128
                            mm = product(d[:, 0:HALF], wqkv_h[:, at:at + 128], wqkv_l[:, at:at + 128],
                                         hnT_h[:, k, u * HALF:(u + 1) * HALF], hnT_l[:, k, u * HALF:(u + 1) * HALF],
                                         k == 0, k == MC - 1)
                        mm.then_inc(dense_full[b], 1)
                    for n, tiles in enumerate(PAIRS):
                        b, d = begin(part, "V", n, g)
                        for t in tiles:
                            for k in range(MC):
                                at = k * 3 * C + 2 * C
                                mm = product(d[:, (t % 2) * 256:(t % 2) * 256 + 256],
                                             hnT_h[:, k, t * 128:t * 128 + 128], hnT_l[:, k, t * 128:t * 128 + 128],
                                             wqkv_h[:, at:at + C], wqkv_l[:, at:at + C], k == 0, k == MC - 1)
                        mm.then_inc(dense_full[b], 1)

                def scores(part, g):
                    wait_read(pe, part, "Q", 7, g)
                    settle(pe)
                    for hq in range(HQ):
                        for t in range(TILES):
                            for hc in range(MC):
                                for b in range(4):
                                    cols = slice(t * 128 + b * POS, t * 128 + b * POS + POS)
                                    at = (t * MC + hc) * POS
                                    mm = pe.matmul(att[hq][b * 32:b * 32 + 32, at:at + POS],
                                                   qT[hq * 32:hq * 32 + 32, hc, cols],
                                                   kT[hq * 32:hq * 32 + 32, hc, cols], start=True, stop=True,
                                                   tile_position=(hq * 32, b * 32))
                        mm.then_inc(scores_ready, 1)

                def attend(part, g):
                    wait_read(pe, part, "V", 3, g)
                    pe.wait_ge(pT_ready, g + 1)
                    settle(pe)
                    for b in range(4):
                        for t in range(TILES):
                            for hc in range(MC):
                                for hq in range(HQ):
                                    h = hc * HQ + hq
                                    at = (t * MC + hc) * POS
                                    idx = (hq * TILES + t) * MC + hc
                                    mm = pe.matmul(att[b][hq * 32:hq * 32 + 32, at:at + POS],
                                                   v[b * 32:b * 32 + 32, t, h * DH:h * DH + DH],
                                                   pT[b * 32:b * 32 + 32, idx, :], start=True, stop=True,
                                                   tile_position=(b * 32, hq * 32))
                        mm.then_inc(attended, 1)

                def project(part, g):
                    pe.wait_ge(oT_lo, g * 4 + 4)
                    for n, tiles in enumerate(PAIRS):
                        b, d = begin(part, "O", n, g)
                        for t in tiles:
                            o = d[:, (t % 2) * 256:(t % 2) * 256 + 256]
                            for m in range(MC):
                                product(o, oT_h[:, t, m, :], oT_l[:, t, m, :],
                                        wo_h[:, m * C:(m + 1) * C], wo_l[:, m * C:(m + 1) * C], m == 0, False)
                            mm = pe.matmul(o, windows[:, t * 128:t * 128 + 128], bouts[:, :], start=False, stop=True)
                        mm.then_inc(dense_full[b], 1)

                def gates(part, g):
                    wait_read(pe, part, "L", 3, g)
                    for t in range(TILES):
                        o = att[0][:, t * E:(t + 1) * E]
                        for m in range(MC):
                            pe.matmul(o, hn2T[:, m, t * 128:t * 128 + 128], wgs[:, m, :], start=(m == 0), stop=False)
                        mm = pe.matmul(o, ones[:, :], bgs[:, :], start=False, stop=True)
                    mm.then_inc(gates_done, 1)

                pe.wait_ge(setup, 2)
                pe.wait_ge(consts_in, 16 * 11)
                transpose_patches("first", 0)
                pe.wait_ge(weights_split, 6)
                embed("first", 0)
                h_to_positions("first", 0, 0)
                hn_to_channels("first", 0, 0)
                with pe.Fori(0, G - 1) as g:
                    qkv("loop", g)
                    transpose_patches("loop", g + 1)
                    scores("loop", g)
                    embed("loop", g + 1)
                    attend("loop", g)
                    h_to_positions("loop", g + 1, g)
                    project("loop", g)
                    hn_to_channels("loop", g + 1, g)
                    hn2_to_channels("loop", g)
                    gates("loop", g)
                qkv("last", G - 1)
                scores("last", G - 1)
                attend("last", G - 1)
                project("last", G - 1)
                hn2_to_channels("last", G - 1)
                gates("last", G - 1)

            @block.scalar
            def _(act):
                def full(part, stage, n, g):
                    b, turns = fill(part, stage, n, g)
                    act.wait_ge(dense_full[b], turns + 1)
                    return b, dense[b]

                def patches_high(part, p, at):
                    for n, (c, w0, nw) in enumerate(TSTEPS):
                        b, d = full(part, "T", n, at)
                        src, dst = patch_views(d, xT_h, c, w0, nw)
                        act.activation(dst, src, ACT.Copy).then_inc(xT_hi, 1)

                def embed_out(part, p, at, ns):
                    if part != "first":
                        act.wait_ge(hn2T_stored, at * 16 + 1)
                    for n in ns:
                        u, m = divmod(n, MC)
                        b, d = full(part, "E", n, at)
                        act.activation(hT[:, m, u * HALF:(u + 1) * HALF], d[:, 0:HALF], ACT.Identity,
                                       bias=bps[:, m:m + 1]).then_inc(dense_free[b], 1)

                def h_out(part, p, at):
                    if part != "first":
                        act.wait_ge(hres_copied, p)
                    for n, tiles in enumerate(PAIRS):
                        b, d = full(part, "F", n, at)
                        act.activation(view(hpos[:, tiles[0], 0:1], [1, 256 * len(tiles)]), d[:, 0:256 * len(tiles)],
                                       ACT.Copy).then_inc(dense_free[b], 1)

                def hn_high(part, p, at):
                    for n, tiles in enumerate(PAIRS):
                        b, d = full(part, "N", n, at)
                        src, dst = channel_views(d, hnT_h, tiles)
                        act.activation(dst, src, ACT.Copy).then_inc(hnT_hi, 1)

                def q_out(part, g):
                    for n in range(4):
                        m, u = divmod(n, 2)
                        b, d = full(part, "Q", n, g)
                        act.activation(qT[:, m, u * HALF:(u + 1) * HALF], d[:, 0:HALF], ACT.Copy).then_inc(dense_free[b], 1)

                def v_out(part, g):
                    for n, tiles in enumerate(PAIRS):
                        b, d = full(part, "V", n, g)
                        act.activation(view(v[:, tiles[0], 0:1], [1, 256 * len(tiles)]), d[:, 0:256 * len(tiles)],
                                       ACT.Copy).then_inc(dense_free[b], 1)

                def softmax_exp(g):
                    act.wait_ge(shifted, g + 1)
                    w = view(win[:, 0, 0, 0:1], [1, 2 * IDX * 6])
                    act.activation(w, w, ACT.Exp, scale=SCALE).then_inc(exped, 1)

                def attended_high(g):
                    for b in range(4):
                        act.wait_ge(attended, g * 4 + b + 1)
                        dst = oT_h[:, :, :, b * POS:(b + 1) * POS].rearrange("p t m i -> p (t m) i")
                        act.activation(dst, att[b][:, 0:TILES * MC * POS].rearrange("p (k i) -> p k i", i=POS),
                                       ACT.Copy).then_inc(oT_hi, 1)

                def hn2_out(part, g):
                    act.wait_ge(hn2T_stored, g * 16 + 1)
                    for n, tiles in enumerate(PAIRS):
                        b, d = full(part, "L", n, g)
                        src, dst = channel_views(d, hn2T, tiles)
                        act.activation(dst, src, ACT.Copy).then_inc(dense_free[b], 1)

                def gate_exp(g):
                    act.wait_ge(gshifted, g + 1)
                    w = view(gate[:, 0, 0:1], [1, TILES * E])
                    act.activation(w, w, ACT.Exp).then_inc(gexped, 1)

                act.wait_ge(weights_in, 48)
                act.activation(wp_h[:, :], view(hpos[:, 0, 0:1], [1, KC * C]), ACT.Copy).then_inc(weights_split, 1)
                act.activation(wqkv_h[:, :], view(hT[:, 0, 0:1], [1, MC * 3 * C]), ACT.Copy).then_inc(weights_split, 1)
                act.activation(wo_h[:, :], view(hn[:, 0, 0:1], [1, MC * C]), ACT.Copy).then_inc(weights_split, 1)
                act.wait_ge(consts_in, 16 * 11)
                patches_high("first", 0, 0)
                act.wait_ge(weights_split, 6)
                embed_out("first", 0, 0, range(4))
                h_out("first", 0, 0)
                hn_high("first", 0, 0)
                with act.Fori(0, G - 1) as g:
                    q_out("loop", g)
                    v_out("loop", g)
                    patches_high("loop", g + 1, g)
                    embed_out("loop", g + 1, g, range(2))
                    softmax_exp(g)
                    embed_out("loop", g + 1, g, range(2, 4))
                    attended_high(g)
                    h_out("loop", g + 1, g)
                    hn_high("loop", g + 1, g)
                    hn2_out("loop", g)
                    gate_exp(g)
                q_out("last", G - 1)
                v_out("last", G - 1)
                softmax_exp(G - 1)
                attended_high(G - 1)
                hn2_out("last", G - 1)
                gate_exp(G - 1)

            @block.vector
            def _(dve):
                ln = [Steps(dve, ln_step[n], 3) for n in range(2)]
                soft = Steps(dve, soft_step, 9)
                gs = Steps(dve, gate_step, 9)

                def full(part, stage, n, g):
                    b, turns = fill(part, stage, n, g)
                    dve.wait_ge(dense_full[b], turns + 1)
                    return b, dense[b]

                def patches_low(part, p, at):
                    for n, (c, w0, nw) in enumerate(TSTEPS):
                        dve.wait_ge(xT_hi, p * 12 + n + 1)
                        b, d = full(part, "T", n, at)
                        for f in range(2):
                            src = d[:, 0:nw * 2 * ROWS].rearrange("k (w f r) -> k f r w", f=2, r=ROWS)[:, f]
                            hi, lo = (xt[:, 2 * c + f, HALO:HALO + TOK].rearrange("k (r w) -> k r w", w=SIDE)[:, :, w0:w0 + nw]
                                      for xt in (xT_h, xT_l))
                            ins = dve.tensor_tensor(lo, src, hi.bitcast(F32), ALU.subtract)
                        ins.then_inc(dense_free[b], 1)

                def statistics(n, g, src):
                    s = ln[n]
                    s.group(g)
                    for t in range(TILES):
                        ins = dve.bn_stats(stat[n][:, t, :], src[:, t, :])
                    s.did(ins)
                    s.wait()
                    settle(dve)
                    for t in range(TILES):
                        ins = dve.bn_aggr(mv[n][:, t, :], stat[n][:, t, :])
                    s.did(ins)
                    s.wait()
                    dve.tensor_scalar(vare[n][:, :], mv[n][:, :, 1], LN_EPS, None, ALU.add).then_inc(var_ready[n], 1)

                def normalise(n, g, src, dst, ready):
                    s = ln[n]
                    dve.wait_ge(rstd_ready[n], g + 1)
                    s.did(dve.scalar_tensor_tensor(shift[n][:, :], mv[n][:, :, 0], -1.0, rstd[n][:, :], ALU.mult, ALU.mult))
                    s.wait()
                    for t in range(TILES):
                        ins = dve.tensor_scalar(dst[:, t, :], src[:, t, :], rstd[n][:, t:t + 1], shift[n][:, t:t + 1],
                                                ALU.mult, ALU.add)
                        if t % 2 or t == TILES - 1:
                            ins.then_inc(ready, 1)
                    s.end()

                def hn_low(part, p, at):
                    for n, tiles in enumerate(PAIRS):
                        dve.wait_ge(hnT_hi, p * 4 + n + 1)
                        b, d = full(part, "N", n, at)
                        src, hi = channel_views(d, hnT_h, tiles)
                        lo = channel_views(d, hnT_l, tiles)[1]
                        dve.tensor_tensor(lo, src, hi.bitcast(F32), ALU.subtract).then_inc(dense_free[b], 1)

                def k_out(part, g):
                    for n in range(4):
                        m, u = divmod(n, 2)
                        b, d = full(part, "Q", 4 + n, g)
                        dve.tensor_copy(kT[:, m, u * HALF:(u + 1) * HALF], d[:, 0:HALF]).then_inc(dense_free[b], 1)

                def softmax(g):
                    s = soft
                    s.group(g)
                    for hq in range(HQ):
                        dve.wait_ge(scores_ready, g * 4 + hq + 1)
                        n = TILES * MC
                        ins = dve.tensor_tensor(banded[:, hq * n:(hq + 1) * n, 0:POS],
                                                att[hq][:, 0:n * POS].rearrange("p (k j) -> p k j", j=POS),
                                                view(band[:, 0:1], [0, n], [1, POS]), ALU.mult)
                    s.did(ins)
                    s.wait()
                    s.did(dve.tensor_reduce(six[:, :, :], view(banded[:, 0, 0:1], [BAND, IDX], [1, 6], [6, BAND // 6]),
                                            AX.X, ALU.add))
                    s.wait()
                    for w in range(2):
                        ins = dve.tensor_tensor(win[:, w], six[:, :, :], view(window[:, 6 * w:6 * w + 1], [0, IDX], [1, 6]), ALU.add)
                    s.did(ins)
                    s.wait()
                    flat = view(win[:, 0, 0, 0:1], [6, 2 * IDX], [1, 6])
                    per = view(wstat[:, 0:1], [1, 2 * IDX], [0, 6])
                    s.did(dve.tensor_reduce(wstat[:, :], flat, AX.X, ALU.max))
                    s.wait()
                    dve.tensor_tensor(flat, flat, per, ALU.subtract).then_inc(shifted, 1)
                    dve.wait_ge(exped, g + 1)
                    s.did(dve.tensor_reduce(wstat[:, :], flat, AX.X, ALU.add))
                    s.wait()
                    s.did(dve.reciprocal(wstat[:, :], wstat[:, :]))
                    s.wait()
                    s.did(dve.tensor_tensor(wstat[:, :], wstat[:, :], there[:, :], ALU.mult))
                    s.wait()
                    s.did(dve.tensor_tensor(flat, flat, per, ALU.mult))
                    s.wait()
                    s.did(dve.tensor_tensor(prob[:, :, :], win[:, 0], win[:, 1], ALU.add))
                    s.wait()
                    dve.tensor_tensor(view(banded[:, 0, 0:1], [BAND, IDX], [6, BAND // 6], [1, 6]),
                                      view(prob[:, 0, 0:1], [6, IDX], [0, BAND // 6], [1, 6]),
                                      view(band[:, 0:1], [0, IDX], [6, BAND // 6], [1, 6]), ALU.mult).then_inc(spread_done, 1)
                    dve.wait_ge(spread_done, g + 1)
                    dve.transpose(pT[:, :, :], banded[:, :, 0:POS]).then_inc(pT_ready, 1)
                    s.end()

                def attended_low(g):
                    for b in range(4):
                        dve.wait_ge(oT_hi, g * 4 + b + 1)
                        hi, lo = (o[:, :, :, b * POS:(b + 1) * POS].rearrange("p t m i -> p (t m) i") for o in (oT_h, oT_l))
                        dve.tensor_tensor(lo, att[b][:, 0:TILES * MC * POS].rearrange("p (k i) -> p k i", i=POS),
                                          hi.bitcast(F32), ALU.subtract).then_inc(oT_lo, 1)

                def residual(part, g):
                    dve.wait_ge(hres_copied, g + 1)
                    dve.wait_ge(h2_stored, g * 64 + 1)
                    for n, tiles in enumerate(PAIRS):
                        b, d = full(part, "O", n, g)
                        w = [1, 256 * len(tiles)]
                        dve.tensor_tensor(view(h2[:, tiles[0], 0:1], w), d[:, 0:256 * len(tiles)],
                                          view(hres[:, tiles[0], 0:1], w), ALU.add).then_inc(dense_free[b], 1)

                def route_gates(g):
                    s = gs
                    s.group(g)
                    dve.wait_ge(gates_done, g + 1)
                    dve.wait_ge(scoresT_stored, g * 128 + 1)
                    logits = att[0][:, 0:TILES * E].rearrange("p (t e) -> p t e", e=E)
                    s.did(dve.tensor_reduce(gstat[:, 0:TILES], logits, AX.X, ALU.max))
                    s.wait()
                    dve.tensor_tensor(gate[:, :, :], logits, view(gstat[:, 0:1], [1, TILES], [0, E]), ALU.subtract).then_inc(gshifted, 1)
                    dve.wait_ge(gexped, g + 1)
                    s.did(dve.tensor_reduce(gstat[:, 0:TILES], gate[:, :, :], AX.X, ALU.add))
                    s.wait()
                    s.did(dve.reciprocal(gstat[:, TILES:2 * TILES], gstat[:, 0:TILES]))
                    s.wait()
                    s.did(dve.tensor_tensor(gate[:, :, :], gate[:, :, :], view(gstat[:, TILES:TILES + 1], [1, TILES], [0, E]), ALU.mult))
                    s.wait()
                    mine = view(gate[:, 0, 0:1], [E, TILES], [1, E], [0, E])
                    other = view(gate[:, 0, 0:1], [E, TILES], [0, E], [1, E])
                    dve.tensor_tensor(above[:, :, :, :], other, mine, ALU.is_gt)
                    s.did(dve.tensor_tensor(level[:, :, :, :], other, mine, ALU.is_equal))
                    s.wait()
                    flat = lambda a: view(a[:, 0, 0, 0:1], [E * E, TILES], [1, E * E])
                    s.did(dve.tensor_tensor(flat(level), flat(level), view(lower[:, 0:1], [0, TILES], [1, E * E]), ALU.mult))
                    s.wait()
                    s.did(dve.tensor_tensor(flat(above), flat(above), flat(level), ALU.add))
                    s.wait()
                    s.did(dve.tensor_reduce(rank[:, :, :], above[:, :, :, :], AX.X, ALU.add))
                    s.wait()
                    both = view(masked[:, 0:1], [1, TILES * E])
                    s.did(dve.scalar_tensor_tensor(both, view(rank[:, 0, 0:1], [1, TILES * E]), TOPK - 0.5,
                                                   view(gate[:, 0, 0:1], [1, TILES * E]), ALU.is_lt, ALU.mult))
                    s.wait()
                    dve.transpose(scoresT[:, :], masked[:, :]).then_inc(scoresT_ready, 1)
                    s.end()

                for n, (hi, lo, src) in enumerate(((wp_h, wp_l, view(hpos[:, 0, 0:1], [1, KC * C])),
                                                   (wqkv_h, wqkv_l, view(hT[:, 0, 0:1], [1, MC * 3 * C])),
                                                   (wo_h, wo_l, view(hn[:, 0, 0:1], [1, MC * C])))):
                    dve.wait_ge(weights_split, 3)
                    dve.tensor_tensor(lo[:, :], src, hi[:, :].bitcast(F32), ALU.subtract).then_inc(weights_split, 1)
                dve.wait_ge(setup, 2)
                dve.wait_ge(consts_in, 16 * 11)
                patches_low("first", 0, 0)
                wait_read(dve, "first", "F", 3, 0)
                statistics(0, 0, hpos)
                normalise(0, 0, hpos, hn, hn_ready)
                hn_low("first", 0, 0)
                with dve.Fori(0, G - 1) as g:
                    k_out("loop", g)
                    patches_low("loop", g + 1, g)
                    softmax(g)
                    attended_low(g)
                    wait_read(dve, "loop", "F", 3, g)
                    statistics(0, g + 1, hpos)
                    normalise(0, g + 1, hpos, hn, hn_ready)
                    residual("loop", g)
                    hn_low("loop", g + 1, g)
                    wait_read(dve, "loop", "O", 3, g)
                    statistics(1, g, h2)
                    normalise(1, g, h2, hn2, hn2_ready)
                    route_gates(g)
                k_out("last", G - 1)
                softmax(G - 1)
                attended_low(G - 1)
                residual("last", G - 1)
                wait_read(dve, "last", "O", 3, G - 1)
                statistics(1, G - 1, h2)
                normalise(1, G - 1, h2, hn2, hn2_ready)
                route_gates(G - 1)

        scores_in = [sem(f"scores_in{c}") for c in range(CH)]
        summed, route_step, picked_ready, picked_stored = sem("summed"), sem("route_step"), sem("picked_ready"), sem("picked_stored")
        ffn_in = sem("ffn_in")

        with nc.Block() as block:
            def rows(dram, c):
                return bass.AP(dram.tensor, dram.offset + c * CIMG * SEQ, [[SEQ, CIMG], [NTOK, E], [1, SEQ]])

            @block.sync
            def _(sp):
                for c in range(CH):
                    sp.dma_start(route[:, c, 0:SEQ], rows(score_d, c)).then_inc(scores_in[c], 16)
                for dst, src in ((w1s, w1), (w2s, w2), (b1s, b1), (b2s, b2), (spread32, c_spread)):
                    sp.dma_start(dst[:, :], src).then_inc(ffn_in, 16)
                sp.wait_ge(ffn_in, 80)
                sp.wait_ge(picked_ready, 1)
                for c in range(CH):
                    sp.dma_start(rows(mask_d, c), picked[:, c, :]).then_inc(picked_stored, 16)
                sp.wait_ge(picked_stored, CH * 16)

            @block.tensor
            def _(pe):
                for c in range(CH):
                    pe.wait_ge(scores_in[c], 16)
                    mm = pe.matmul(bank[0][:, 0:SEQ], same[:, :], route[:, c, 0:SEQ], start=(c == 0), stop=(c == CH - 1))
                mm.then_inc(summed, 1)

            @block.vector
            def _(dve):
                s = Steps(dve, route_step, 4 + 2 * (PICK + PAD) // 8)
                s.group(0)
                dve.memset(route[:, :, SEQ:SEQ + PAD], BIG)
                dve.wait_ge(summed, 1)
                s.did(dve.tensor_scalar(rden[:, :], bank[0][:, 0:SEQ], GATE_EPS, None, ALU.add))
                s.wait()
                s.did(dve.reciprocal(rden[:, :], rden[:, :]))
                s.wait()
                s.did(dve.scalar_tensor_tensor(route[:, :, 0:SEQ], route[:, :, 0:SEQ], float(B),
                                               view(rden[:, 0:1], [0, CH], [1, SEQ]), ALU.mult, ALU.mult))
                s.wait()
                for _ in range((PICK + PAD) // 8):
                    for c in range(CH):
                        ins = dve.max(best[:, c, :], route[:, c, :])
                    s.did(ins)
                    s.wait()
                    for c in range(CH):
                        ins = dve.match_replace(route[:, c, :], best[:, c, :], route[:, c, :], -1.0)
                    s.did(ins)
                    s.wait()
                dve.tensor_scalar(picked[:, :, :], route[:, :, 0:SEQ], 0.0, None, ALU.is_lt).then_inc(picked_ready, 1)
                dve.wait_ge(ffn_in, 80)
                s.did(dve.tensor_copy(spread[:, :], spread32[:, :]))
                s.end()

            @block.scalar
            def _(act):
                pass

            @block.gpsimd
            def _(pool):
                pass

        w_high, w_low = sem("w_high"), sem("w_low")
        t_in_loaded, t_high, t_low = sem("t_in_loaded"), sem("t_high"), sem("t_low")
        mask_loaded, mask_copied = sem("mask_loaded"), sem("mask_copied")
        h_loaded, y_full, y_added, y_stored = sem("h_loaded"), sem("y_full"), sem("y_added"), sem("y_stored")
        hid_full, activated = sem("hid_full"), sem("activated")
        spread_full, mask_put = sem("spread_full"), sem("mask_put")
        hid_high, hid_low = sem("hid_high"), sem("hid_low")
        UT = TOK // 2
        STEPS3 = [(u, c) for u in range(2) for c in range(HID)]
        N3 = len(STEPS3)
        out_t = out.rearrange("(g t p) n -> g p t n", t=TILES, p=4 * Q)

        with nc.Block() as block:
            @block.sync
            def _(sp):
                def load_t(i):
                    sp.dma_start(view(t_in[:, 0, 0:1], [1, MC * GPOS]), h2n_d[i]).then_inc(t_in_loaded, 16)

                def load_mask(i):
                    sp.dma_start(mask16[:, :], mask_d[:, bass.ds(i * TOK, TOK)]).then_inc(mask_loaded, 16)

                def load_h(i):
                    sp.dma_start(h_in[:, :, :], out_t[i]).then_inc(h_loaded, 16)

                def store(i):
                    sp.wait_ge(y_added, i * 4 + 4)
                    sp.dma_start(out_t[i], y_out[:, :, :]).then_inc(y_stored, 16)

                sp.sem_inc(y_stored, 1)
                load_t(0)
                load_mask(0)
                load_h(0)
                with sp.Fori(0, G - 1) as i:
                    sp.wait_ge(t_low, i + 1)
                    load_t(i + 1)
                    sp.wait_ge(mask_copied, i + 1)
                    sp.wait_ge(mask_put, i * N3 + N3)
                    load_mask(i + 1)
                    store(i)
                    load_h(i + 1)
                store(G - 1)
                sp.wait_ge(y_stored, G * 16 + 1)

            @block.tensor
            def _(pe):
                def product(o, a_h, a_l, b_h, b_l, start, stop):
                    pe.matmul(o, a_h, b_h, start=start, stop=False)
                    pe.matmul(o, a_l, b_h, start=False, stop=False)
                    return pe.matmul(o, a_h, b_l, start=False, stop=stop)

                def hidden(i):
                    pe.wait_ge(t_low, i + 1)
                    pe.wait_ge(mask_loaded, i * 16 + 16)
                    for n, (u, c) in enumerate(STEPS3):
                        if n >= 2:
                            pe.wait_ge(activated, i * N3 + n - 1)
                        for k in range(MC):
                            at = k * E * SUB + c * 128
                            at_t = u * HALF + HALO
                            th, tl = (view(t[:, k, at_t:at_t + 1], [POS, BLOCKS // 2], [1, Q]) for t in (t_h, t_l))
                            mm = product(bank[n % 2][:, 0:UT], w1_h[:, at:at + 128], w1_l[:, at:at + 128], th, tl,
                                         k == 0, k == MC - 1)
                        mm.then_inc(hid_full, 1)
                        if n >= 2:
                            pe.wait_ge(mask_put, i * N3 + n - 1)
                        pe.matmul(bank[2 + n % 2][:, 0:UT], spread[:, c * 128:(c + 1) * 128],
                                  mask16[:, u * UT:(u + 1) * UT], start=True, stop=True).then_inc(spread_full, 1)

                def outputs(i):
                    pe.wait_ge(mask_copied, i + 1)
                    for n, tiles in enumerate(PAIRS):
                        pe.wait_ge(hid_low, i * N3 + (HID if n == 0 else N3))
                        for t in tiles:
                            o = bank[4 + n][0:4 * Q, (t % 2) * 256:(t % 2) * 256 + 256]
                            cols = slice(t * 4 * Q, (t + 1) * 4 * Q)
                            for c in range(HID):
                                product(o, hid_h[:, c, cols], hid_l[:, c, cols], w2_h[:, c * C:(c + 1) * C],
                                        w2_l[:, c * C:(c + 1) * C], c == 0, False)
                            mm = pe.matmul(o, mask32[:, cols], b2s[:, :], start=False, stop=True)
                        mm.then_inc(y_full, 1)

                pe.wait_ge(w_low, 2)
                with pe.Fori(0, G) as i:
                    hidden(i)
                    outputs(i)

            @block.scalar
            def _(act):
                def split_high(i):
                    act.wait_ge(t_in_loaded, i * 16 + 16)
                    act.activation(t_h[:, :, :], t_in[:, :, :], ACT.Copy).then_inc(t_high, 1)

                def high(i, n):
                    u, c = STEPS3[n]
                    act.wait_ge(mask_put, i * N3 + n + 1)
                    act.activation(hid_h[:, c, u * UT:(u + 1) * UT], hid[:, c, u * UT:(u + 1) * UT],
                                   ACT.Copy).then_inc(hid_high, 1)

                def group(i):
                    for n, (u, c) in enumerate(STEPS3):
                        act.wait_ge(hid_full, i * N3 + n + 1)
                        act.activation(hid[:, c, u * UT:(u + 1) * UT], bank[n % 2][:, 0:UT], ACT.Gelu,
                                       bias=b1s[:, c:c + 1]).then_inc(activated, 1)
                        if n > 0:
                            high(i, n - 1)
                    high(i, N3 - 1)

                act.activation(w1_h[:, :], w1s[:, :], ACT.Copy).then_inc(w_high, 1)
                act.activation(w2_h[:, :], w2s[:, :], ACT.Copy).then_inc(w_high, 1)
                split_high(0)
                with act.Fori(0, G - 1) as i:
                    group(i)
                    split_high(i + 1)
                group(G - 1)

            @block.vector
            def _(dve):
                def split_low(i):
                    dve.wait_ge(t_high, i + 1)
                    dve.tensor_tensor(t_l[:, :, :], t_in[:, :, :], t_h[:, :, :].bitcast(F32), ALU.subtract).then_inc(t_low, 1)

                def low(i, n):
                    u, c = STEPS3[n]
                    cols = slice(u * UT, (u + 1) * UT)
                    dve.wait_ge(hid_high, i * N3 + n + 1)
                    dve.tensor_tensor(hid_l[:, c, cols], hid[:, c, cols], hid_h[:, c, cols].bitcast(F32),
                                      ALU.subtract).then_inc(hid_low, 1)

                def group(i):
                    dve.wait_ge(mask_loaded, i * 16 + 16)
                    dve.tensor_copy(mask32[:, :], mask16[:, :]).then_inc(mask_copied, 1)
                    for n, (u, c) in enumerate(STEPS3):
                        cols = slice(u * UT, (u + 1) * UT)
                        dve.wait_ge(activated, i * N3 + n + 1)
                        dve.wait_ge(spread_full, i * N3 + n + 1)
                        dve.tensor_tensor(hid[:, c, cols], bank[2 + n % 2][:, 0:UT], hid[:, c, cols],
                                          ALU.mult).then_inc(mask_put, 1)
                        if n > 0:
                            low(i, n - 1)
                    low(i, N3 - 1)

                def add(i):
                    dve.wait_ge(h_loaded, i * 16 + 16)
                    dve.wait_ge(y_stored, i * 16 + 1)
                    for n, tiles in enumerate(PAIRS):
                        dve.wait_ge(y_full, i * 4 + n + 1)
                        w = [1, 256 * len(tiles)]
                        dve.tensor_tensor(view(y_out[:, tiles[0], 0:1], w), bank[4 + n][0:4 * Q, 0:256 * len(tiles)],
                                          view(h_in[:, tiles[0], 0:1], w), ALU.add).then_inc(y_added, 1)

                for n, (hi, lo, src) in enumerate(((w1_h, w1_l, w1s), (w2_h, w2_l, w2s))):
                    dve.wait_ge(w_high, n + 1)
                    dve.tensor_tensor(lo[:, :], src[:, :], hi[:, :].bitcast(F32), ALU.subtract).then_inc(w_low, 1)
                split_low(0)
                with dve.Fori(0, G - 1) as i:
                    group(i)
                    split_low(i + 1)
                    add(i)
                group(G - 1)
                add(G - 1)

            @block.gpsimd
            def _(pool):
                pass


_OUT = "out_dram"


def kernel(x, L0_tok_W, L0_tok_b, L0_attn_w_qkv, L0_attn_w_out, L0_attn_b_out, L0_ffn_w_gate_w, L0_ffn_w_gate_b,
           L0_ffn_W1, L0_ffn_b1, L0_ffn_W2, L0_ffn_b2):
    import numpy as np
    import concourse.bacc as bacc
    from concourse.bass_utils import run_bass_kernel_spmd

    def chunks(a):
        a = np.asarray(a)
        return a.reshape(-1, 128, a.shape[1]).transpose(1, 0, 2).reshape(128, -1)

    arrays = {
        "x": x, "w_patch": chunks(np.asarray(L0_tok_W).T), "b_patch": np.asarray(L0_tok_b).reshape(MC, 128).T,
        "w_qkv": chunks(L0_attn_w_qkv), "w_out": chunks(L0_attn_w_out), "b_out": np.asarray(L0_attn_b_out).reshape(1, C),
        "w_gate": chunks(L0_ffn_w_gate_w), "b_gate": np.asarray(L0_ffn_w_gate_b).reshape(1, E),
        "w1": chunks(np.asarray(L0_ffn_W1).transpose(1, 0, 2).reshape(C, E * SUB)),
        "b1": np.asarray(L0_ffn_b1).reshape(HID, 128).T,
        "w2": chunks(np.asarray(L0_ffn_W2).reshape(E * SUB, C)), "b2": np.asarray(L0_ffn_b2),
    }
    arrays.update(shape_constants(np))
    arrays = {name: np.ascontiguousarray(a) for name, a in arrays.items()}
    B = arrays["x"].shape[0]
    nc = bacc.Bacc("TRN2", target_bir_lowering=False, num_devices=1)
    args = [nc.dram_tensor(f"in_{name}", a.shape, mybir.dt.from_np(a.dtype), kind="ExternalInput").ap()
            for name, a in arrays.items()]
    args.append(nc.dram_tensor(_OUT, (B * SEQ, C), F32, kind="ExternalOutput").ap())
    vit_layer(nc, *args)
    r = run_bass_kernel_spmd(nc, [{f"in_{name}": a for name, a in arrays.items()}], core_ids=[0])
    return r.results[0][_OUT].reshape(B, SEQ, C)
```

```python
from contextlib import ExitStack

import concourse.bass as bass
from concourse import mybir

F32 = mybir.dt.float32
F32R = mybir.dt.float32r
BF16 = mybir.dt.bfloat16
ALU = mybir.AluOpType
ACT = mybir.ActivationFunctionType
AX = mybir.AxisListType

C = 256
MC = C // 128
PATCH = 16
SIDE = 14
SEQ = SIDE * SIDE
IMG = 4
ROWS = IMG * SIDE
TOK = IMG * SEQ
HEADS, DH, KS, STRIDE = 8, 32, 4, 2
HALO = STRIDE
POS = 32
Q = POS - 2 * HALO
BLOCKS = TOK // Q
TILES = BLOCKS // 4
GPOS = BLOCKS * POS
HALF = GPOS // 2
BAND = 36
HQ = 4
HIDX = HQ * TILES
IDX = MC * HIDX
E, SUB, TOPK = 8, 64, 2
HID = E * SUB // 128
KC = 3 * PATCH * PATCH // 128
LN_EPS = 1e-5
GATE_EPS = 1e-6
SCALE = float(C) ** -0.5
PICK = SEQ // 2
GAP = 32
ROUNDS = -(-PICK // 8)
GPC = 128 // E // IMG
LOOP_ROUNDS = -(-ROUNDS // GPC) * GPC
PAD = LOOP_ROUNDS * 8 - PICK
BIG = 1e30


def shape_constants(np):
    pos = np.arange(128)
    i = pos % POS
    pair = i // 2
    kap = np.arange(BAND)
    band = ((np.abs(kap[None, :] // 2 - pair[:, None]) <= 1) & (kap[None, :] < POS)).astype(np.float32)
    slot = (np.arange(6) // 2)[None, :]
    out0 = (pair[:, None] + 1) % 3 == slot
    out1 = (pair[:, None] - 1) % 3 == slot
    window = np.stack([np.where(out0, -BIG, 0), np.where(out1, -BIG, 0)], 1).astype(np.float32)
    block = (np.arange(TILES)[None, :] * 4 + (pos // POS)[:, None]) % (SEQ // Q)
    has0 = ~((block == 0) & (pair[:, None] == 1))
    has1 = ~((block == SEQ // Q - 1) & (pair[:, None] == POS // 2 - 2))
    has = np.stack([has0, has1], 1).astype(np.float32)
    there = np.broadcast_to(has[:, :, None, :], (128, 2, HQ, TILES)).reshape(128, 2 * HIDX)
    windows = has.sum(1)
    e = np.arange(E)
    lower = np.broadcast_to((e[None, :] < e[:, None]).reshape(1, E * E), (128, E * E))
    same = (pos[:, None] % E == pos[None, :] % E)
    spread = np.zeros((E, HID * 128), np.float32)
    for c in range(HID):
        for m in range(128):
            spread[(c * 128 + m) // SUB, c * 128 + m] = 1
    f = lambda a: np.ascontiguousarray(a, dtype=np.float32)
    return {"c_ident": f(np.eye(128)), "c_band": f(band), "c_window": f(window.reshape(128, 12)),
            "c_there": f(there), "c_windows": f(windows), "c_lower": f(lower), "c_same": f(same),
            "c_spread": f(spread)}


class Steps:

    def __init__(self, eng, sem, per_group):
        self.eng, self.sem, self.per_group = eng, sem, per_group

    def group(self, g):
        self.base, self.n = g * self.per_group, 0

    def did(self, ins):
        ins.then_inc(self.sem, 1)
        self.n += 1

    def wait(self):
        self.eng.wait_ge(self.sem, self.base + self.n)

    def end(self):
        assert self.n == self.per_group, self.n


def vit_layer(nc, x, w_patch, b_patch, w_qkv, w_out, b_out, w_gate, b_gate, w1, b1, w2, b2,
              c_ident, c_band, c_window, c_there, c_windows, c_lower, c_same, c_spread, out):
    B = x.shape[0]
    G = B // IMG
    NTOK = B * SEQ
    CH = B * E // 128
    CIMG = 128 // E

    h2n_d = nc.dram_tensor("normalised_tokens", (G, 128, TILES * C), F32, kind="Internal").ap()
    score_d = nc.dram_tensor("gate_scores", (E, NTOK), F32, kind="Internal").ap()
    mask_d = nc.dram_tensor("picked", (E, NTOK), BF16, kind="Internal").ap()

    def view(ap, *dims):
        return bass.AP(ap.tensor, ap.offset, [list(ap.ap[0])] + [list(d) for d in dims])

    weights = ExitStack()
    with weights:
        def tensor(stack, name, shape, dt=F32):
            return stack.enter_context(nc.sbuf_tensor(name, shape, dt))

        def sem(name):
            return weights.enter_context(nc.semaphore(name))

        bank = [weights.enter_context(nc.psum_tensor(f"bank{n}", [128, 512], F32)) for n in range(8)]
        att, dense = bank[:4], bank[4:]

        ident = tensor(weights, "ident", [128, 128])
        same = tensor(weights, "same", [128, 128])
        b1s = tensor(weights, "b1s", [128, HID])
        b2_left = tensor(weights, "b2_left", [3 * GAP, C])
        b2_parts = tensor(weights, "b2_parts", [3 * GAP, C], BF16)
        spread32 = tensor(weights, "spread32", [E, HID * 128])
        spread = tensor(weights, "spread", [E, HID * 128], BF16)

        one = ExitStack()
        band = tensor(one, "band", [128, BAND])
        window = tensor(one, "window", [128, 12])
        there = tensor(one, "there", [128, 2 * HIDX])
        windows = tensor(one, "windows", [128, TILES])
        lower = tensor(one, "lower", [128, E * E])
        b_embed = tensor(one, "b_embed", [128, C])
        b_attn = tensor(one, "b_attn", [128, TILES, C])
        wgs = tensor(one, "wgs", [128, MC, E])
        bgs = tensor(one, "bgs", [1, TILES, E])
        ones = tensor(one, "ones", [1, 128])
        eps = tensor(one, "eps", [128, 2 * TILES])
        wp_h = tensor(one, "wp_h", [128, KC * C], F32R)
        wp_l = tensor(one, "wp_l", [128, KC * C], F32R)
        wqkv_h = tensor(one, "wqkv_h", [128, MC * 3 * C], F32R)
        wqkv_l = tensor(one, "wqkv_l", [128, MC * 3 * C], F32R)
        wo_h = tensor(one, "wo_h", [128, MC * C], F32R)
        wo_l = tensor(one, "wo_l", [128, MC * C], F32R)
        raw = tensor(one, "raw", [2 * ROWS, 8 * SIDE * PATCH])
        patches = tensor(one, "patches", [2 * ROWS, 3, SIDE, 128])
        xT_h = tensor(one, "xT_h", [128, KC, GPOS], F32R)
        xT_l = tensor(one, "xT_l", [128, KC, GPOS], F32R)
        hpos = tensor(one, "hpos", [128, TILES, C])
        hn = tensor(one, "hn", [128, TILES, C])
        hnT_h = tensor(one, "hnT_h", [128, MC, GPOS], F32R)
        hnT_l = tensor(one, "hnT_l", [128, MC, GPOS], F32R)
        qT = tensor(one, "qT", [128, MC, GPOS])
        kT = tensor(one, "kT", [128, MC, GPOS])
        v = tensor(one, "v", [128, TILES, C])
        banded = tensor(one, "banded", [128, IDX, BAND])
        six = tensor(one, "six", [128, IDX, 6])
        win = tensor(one, "win", [128, MC, 2, HIDX, 6])
        wstat = tensor(one, "wstat", [128, MC, 2 * HIDX])
        prob = tensor(one, "prob", [128, IDX, 6])
        oT_h = tensor(one, "oT_h", [128, TILES, MC, 128], F32R)
        oT_l = tensor(one, "oT_l", [128, TILES, MC, 128], F32R)
        h2 = tensor(one, "h2", [128, TILES, C])
        hn2 = hn
        hn2T = tensor(one, "hn2T", [128, MC, GPOS])
        stat = [tensor(one, f"stat{n}", [128, TILES, 6]) for n in range(2)]
        mv = [tensor(one, f"mv{n}", [128, TILES, 2]) for n in range(2)]
        vare = [tensor(one, f"vare{n}", [128, TILES]) for n in range(2)]
        rstd = [tensor(one, f"rstd{n}", [128, TILES]) for n in range(2)]
        negmean = [tensor(one, f"negmean{n}", [128, TILES]) for n in range(2)]
        shift = [tensor(one, f"shift{n}", [128, TILES]) for n in range(2)]
        gate = tensor(one, "gate", [128, TILES, E])
        gstat = tensor(one, "gstat", [128, 2 * TILES])
        above = view(win[:, 0, 0, 0, 0:1], [E * E, TILES], [E, E], [1, E])
        level = tensor(one, "level", [128, TILES, E, E])
        rank = tensor(one, "rank", [128, TILES, E])
        masked = tensor(one, "masked", [128, 64])
        scoresT = tensor(one, "scoresT", [128, 64])
        pT = qT[:, :, :].rearrange("p m n -> p (m n)").rearrange("p (k j) -> p k j", j=POS)
        one.close()

        route = tensor(weights, "route", [128, CH, SEQ + PAD])
        rden = tensor(weights, "rden", [128, SEQ])
        best = tensor(weights, "best", [128, CH, 8])
        picked = tensor(weights, "picked_sb", [128, CH, SEQ], BF16)

        three = ExitStack()
        w1s = tensor(three, "w1s", [128, MC * E * SUB])
        w2s = tensor(three, "w2s", [128, HID * C])
        w1_h = tensor(three, "w1_h", [128, MC * E * SUB], F32R)
        w1_l = tensor(three, "w1_l", [128, MC * E * SUB], F32R)
        w2_h = tensor(three, "w2_h", [128, HID * C], F32R)
        w2_l = tensor(three, "w2_l", [128, HID * C], F32R)
        t_in = tensor(three, "t_in", [128, MC, GPOS])
        t_h = tensor(three, "t_h", [128, MC, GPOS], F32R)
        t_l = tensor(three, "t_l", [128, MC, GPOS], F32R)
        h_in = tensor(three, "h_in", [4 * Q, TILES, C])
        y_out = tensor(three, "y_out", [4 * Q, TILES, C])
        mask16 = tensor(three, "mask16", [3 * GAP, TOK], BF16)
        hid = tensor(three, "hid", [128, HID, TOK])
        hid_h = tensor(three, "hid_h", [128, HID, TOK], F32R)
        hid_l = tensor(three, "hid_l", [128, HID, TOK], F32R)
        three.close()

        def stage(name, *ns):
            return [(name, n) for n in ns]

        T, Q8 = stage("T", *range(12)), stage("Q", *range(8))
        four = {name: stage(name, *range(4)) for name in "NVELO"}
        O4 = four["O"]
        BEGIN = four["N"] + T[4:8] + [fill for pair in zip(Q8[0:4], T[8:12]) for fill in pair] + Q8[4:8] + four["V"]
        FILLS = {"first": T + four["E"],
                 "zero": T[0:4] + BEGIN + four["E"],
                 "loop": T[0:3] + O4[0:2] + T[3:4] + O4[2:4] + BEGIN + four["L"] + four["E"],
                 "last": O4 + four["N"] + Q8 + four["V"] + four["L"],
                 "end": O4 + four["L"]}

        def until(part, name, n):
            return FILLS[part][:FILLS[part].index((name, n))]

        TURNS = {part: len(fills) // 4 for part, fills in FILLS.items()}
        BEFORE = {"first": 0, "zero": TURNS["first"], "loop": TURNS["first"] + TURNS["zero"]}
        BEFORE["last"] = BEFORE["loop"] + (G - 2) * TURNS["loop"]
        BEFORE["end"] = BEFORE["last"] + TURNS["last"]

        def fill(part, stage, n, g):
            at = FILLS[part].index((stage, n))
            turns = BEFORE[part] + at // 4
            if part == "loop":
                turns = g * TURNS["loop"] + (turns - TURNS["loop"])
            return at % 4, turns

        def wait_read(eng, part, stage, n, g):
            b, turns = fill(part, stage, n, g)
            eng.wait_ge(dense_free[b], turns + 1)

        PAIRS = [(0, 1), (2, 3), (4, 5), (6,)]
        TSTEPS = [(c, w, min(4, SIDE - w)) for c in range(3) for w in range(0, SIDE, 4)]
        assert len(TSTEPS) == 12 and len(PAIRS) == 4
        SOFT_STEPS = 8

        dense_full = [sem(f"dense_full{b}") for b in range(4)]
        dense_free = [sem(f"dense_free{b}") for b in range(4)]
        consts_in = sem("consts_in")
        ident_in = sem("ident_in")
        weight_in = [sem(f"weight_in{n}") for n in range(3)]
        weights_high, weights_low = sem("weights_high"), sem("weights_low")
        setup = sem("setup")
        raw_loaded, patched = [sem(f"raw_loaded{c}") for c in range(3)], sem("patched")
        xT_hi = sem("xT_hi")
        halo_copied = sem("halo_copied")
        h2_begun = sem("h2_begun")
        bias_spread = sem("bias_spread")
        var_ready = [sem(f"var_ready{n}") for n in range(2)]
        rstd_ready = [sem(f"rstd_ready{n}") for n in range(2)]
        shift_ready = [sem(f"shift_ready{n}") for n in range(2)]
        hn_ready = sem("hn_ready")
        hnT_hi = sem("hnT_hi")
        scores_ready, scores_read = sem("scores_ready"), sem("scores_read")
        shifted, exped = sem("shifted"), sem("exped")
        spread_done, pT_ready = sem("spread_done"), sem("pT_ready")
        attended = sem("attended")
        oT_hi, oT_lo = sem("oT_hi"), sem("oT_lo")
        h2_stored = sem("h2_stored")
        hn2_ready = sem("hn2_ready")
        hn2T_stored = sem("hn2T_stored")
        gates_done = sem("gates_done")
        gshifted, gexped = sem("gshifted"), sem("gexped")
        scoresT_ready, scoresT_stored = sem("scoresT_ready"), sem("scoresT_stored")
        ln_step = [sem(f"ln_step{n}") for n in range(2)]
        soft_step, gate_step = sem("soft_step"), sem("gate_step")

        passed = sem("passed")

        def settle(eng):
            eng.sem_inc(passed, 1)

        def patch_views(d, xt, c, w0, nw):
            src = view(d[:, 0:1], [2, 2 * BLOCKS], [1, 2], [2 * ROWS, nw])
            dst = view(xt[:, 2 * c, HALO + w0:HALO + w0 + 1], [POS, 2 * BLOCKS], [SIDE, 2], [1, nw])
            return src, dst

        def attended_views(bank, o, n):
            src = bank[:, 0:MC * TILES * POS].rearrange("p (m t i) -> p m t i", m=MC, i=POS)
            dst = view(o[:, 0, 0, n * POS:n * POS + 1], [128, MC], [MC * 128, TILES], [1, POS])
            return src, dst

        def channel_views(d, a, tiles):
            src = d[:, 0:256 * len(tiles)].rearrange("p (t m c) -> p m t c", m=MC, c=128)
            dst = a[:, :, tiles[0] * 128:(tiles[-1] + 1) * 128].rearrange("p m (t c) -> p m t c", c=128)
            return src, dst

        x_v = x.rearrange("(g b) c (n f r) w -> g f c b n (r w)", b=IMG, n=SIDE, f=2)
        out_v = out.rearrange("(g t b i) n -> g b i t n", t=TILES, b=4, i=Q)

        with nc.Block() as block:
            def copies(row, *counts):
                return bass.AP(row.tensor, row.offset, [[0, n] for n in counts] + [[1, row.shape[-1]]])

            WEIGHTS = ((wp_h, wp_l, view(hpos[:, 0, 0:1], [1, KC * C])),
                       (wqkv_h, wqkv_l, view(hn2T[:, 0, 0:1], [1, MC * 3 * C])),
                       (wo_h, wo_l, view(hn[:, 0, 0:1], [1, MC * C])))
            FIRST_RAW = (raw, *(view(a[:, 0, 0:1], [1, 8 * SIDE * PATCH])[0:2 * ROWS] for a in (h2, v)))

            @block.sync
            def _(sp):
                def load(p, part=None):
                    for c in range(3):
                        to = FIRST_RAW[c] if part == "first" else raw
                        if part == "second" and c == 0:
                            sp.wait_ge(patched, 1)
                        elif part != "first":
                            sp.wait_ge(patched, p * 3 + c)
                        for f in range(2):
                            sp.dma_start(to[f * ROWS:(f + 1) * ROWS, :], x_v[p, f, c]).then_inc(raw_loaded[c], 16)

                def store_h2(part, g, at):
                    wait_read(sp, part, "O", 3, at)
                    for b in range(4):
                        sp.dma_start(out_v[g, b], h2[b * POS + HALO:b * POS + HALO + Q, :, :]).then_inc(h2_stored, 16)

                def store_rest(part, g, at):
                    wait_read(sp, part, "L", 3, at)
                    sp.dma_start(h2n_d[g], view(hn2T[:, 0, 0:1], [1, MC * GPOS])).then_inc(hn2T_stored, 16)
                    sp.wait_ge(scoresT_ready, g + 1)
                    for b in range(4):
                        for half in range(2):
                            tiles = min(4, TILES - 4 * half)
                            at = g * TOK + half * 16 * Q + b * Q
                            dst = bass.AP(score_d.tensor, score_d.offset + at, [[4 * Q, tiles], [NTOK, E], [1, Q]])
                            src = scoresT[b * 32:b * 32 + tiles * E, half * 32 + HALO:half * 32 + HALO + Q]
                            sp.dma_start(dst, src).then_inc(scoresT_stored, 16)

                sp.dma_start(ident[:, :], c_ident).then_inc(ident_in, 16)
                load(0, "first")
                for stored in (h2_stored, hn2T_stored, scoresT_stored):
                    sp.sem_inc(stored, 1)
                load(1, "second")
                load(2)
                with sp.Fori(1, G - 2) as g:
                    load(g + 2)
                    store_h2("loop", g - 1, g)
                    store_rest("loop", g - 1, g)
                store_h2("loop", G - 3, G - 2)
                store_rest("loop", G - 3, G - 2)
                store_h2("last", G - 2, G - 1)
                store_rest("last", G - 2, G - 1)
                store_h2("end", G - 1, G - 1)
                store_rest("end", G - 1, G - 1)
                sp.wait_ge(h2_stored, G * 64 + 1)
                sp.wait_ge(hn2T_stored, G * 16 + 1)
                sp.wait_ge(scoresT_stored, G * 128 + 1)

            @block.gpsimd
            def _(pool):
                pool.memset(ones[:, :], 1.0)
                pool.memset(eps[:, :], -0.5)
                pool.memset(masked[:, :], 0.0)
                pool.memset(banded[:, :, POS:BAND], 0.0)
                for xt in (xT_h, xT_l):
                    pool.memset(xt[:, 0, 0:HALO].bitcast(F32), 0.0)
                    last = pool.memset(xt[:, KC - 1, GPOS - HALO:GPOS].bitcast(F32), 0.0)
                last.then_inc(setup, 1)
                pool.wait_ge(setup, 1)

                def root(n, g):
                    pool.wait_ge(var_ready[n], g + 1)
                    pool.tensor_tensor(rstd[n][:, :], vare[n][:, :], eps[:, 0:TILES], ALU.pow).then_inc(rstd_ready[n], 1)
                    pool.wait_ge(rstd_ready[n], g + 1)
                    pool.tensor_tensor(shift[n][:, :], negmean[n][:, :], rstd[n][:, :], ALU.mult).then_inc(shift_ready[n], 1)

                def begin_h2(g):
                    if not isinstance(g, int) or g > 0:
                        pool.wait_ge(h2_stored, g * 64 + 1)
                        pool.wait_ge(hn2_ready, g * 4)
                        settle(pool)
                    else:
                        pool.wait_ge(bias_spread, 1)
                    pool.tensor_tensor(view(h2[:, 0, 0:1], [1, TILES * C]), view(hpos[:, 0, 0:1], [1, TILES * C]),
                                       view(b_attn[:, 0, 0:1], [1, TILES * C]), ALU.add).then_inc(h2_begun, 1)

                def halo(part, at):
                    wait_read(pool, part, "T", 11, at)
                    settle(pool)
                    n = KC * BLOCKS - 1
                    for xt in (xT_h, xT_l):
                        for to, of in ((POS, Q), (Q + HALO, POS + HALO)):
                            ins = pool.tensor_scalar(view(xt[:, 0, to:to + 1], [POS, n], [1, HALO]),
                                                     view(xt[:, 0, of:of + 1], [POS, n], [1, HALO]).bitcast(F32),
                                                     1.0, 0.0, ALU.mult, ALU.add)
                    ins.then_inc(halo_copied, 1)

                def gather_patches(p, c, part, at):
                    pool.wait_ge(raw_loaded[c], p * 32 + 32)
                    if part is not None:
                        b, turns = fill(part, "T", 4 * c + 3, at)
                        pool.wait_ge(dense_full[b], turns + 1)
                    settle(pool)
                    pool.tensor_scalar(patches[:, c, :, :].rearrange("p w (r i) -> p r w i", i=PATCH),
                                       (raw if part is not None else FIRST_RAW[c])[:, :].rearrange("p (r w i) -> p r w i", r=8, i=PATCH),
                                       1.0, 0.0, ALU.mult, ALU.add).then_inc(patched, 1)

                def iteration(part, g, gathers=True):
                    if gathers:
                        gather_patches(g + 2, 0, part, g)
                        gather_patches(g + 2, 1, part, g)
                    halo(part, g)
                    if part != "zero":
                        root(1, g - 1)
                    if gathers:
                        gather_patches(g + 2, 2, part, g)
                    begin_h2(g)
                    root(0, g + 1)

                for c in range(3):
                    gather_patches(0, c, None, 0)
                halo("first", 0)
                gather_patches(1, 0, "first", 0)
                root(0, 0)
                gather_patches(1, 1, "first", 0)
                gather_patches(1, 2, "first", 0)
                iteration("zero", 0)
                with pool.Fori(1, G - 2) as g:
                    iteration("loop", g)
                iteration("loop", G - 2, gathers=False)
                root(1, G - 2)
                begin_h2(G - 1)
                root(1, G - 1)

            @block.tensor
            def _(pe):
                def begin(part, stage, n, g):
                    b, turns = fill(part, stage, n, g)
                    if not isinstance(turns, int) or turns > 0:
                        pe.wait_ge(dense_free[b], turns)
                    return b, dense[b]

                def product(o, a_h, a_l, b_h, b_l, start, stop):
                    pe.matmul(o, a_h, b_h, start=start, stop=False)
                    pe.matmul(o, a_l, b_h, start=False, stop=False)
                    return pe.matmul(o, a_h, b_l, start=False, stop=stop)

                def transpose_patches(part, p, at, ns):
                    for n in ns:
                        c, w0, nw = TSTEPS[n]
                        if w0 == 0:
                            pe.wait_ge(patched, p * 3 + c + 1)
                        b, d = begin(part, "T", n, at)
                        for w in range(nw):
                            mm = pe.transpose(d[:, w * 2 * ROWS:(w + 1) * 2 * ROWS], patches[:, c, w0 + w, :], ident[0:2 * ROWS, 0:2 * ROWS])
                        mm.then_inc(dense_full[b], 1)

                def embed(part, p, at, t):
                    if t == 0:
                        pe.wait_ge(halo_copied, p + 1)
                    b, _ = fill(part, "E", t // 2, at)
                    if t % 2 == 0:
                        begin(part, "E", t // 2, at)
                    for k in range(KC):
                        mm = product(dense[b][:, (t % 2) * 256:(t % 2) * 256 + 256],
                                     xT_h[:, k, t * 128:t * 128 + 128], xT_l[:, k, t * 128:t * 128 + 128],
                                     wp_h[:, k * C:(k + 1) * C], wp_l[:, k * C:(k + 1) * C],
                                     k == 0, k == KC - 1)
                    if t in (tiles[-1] for tiles in PAIRS):
                        mm.then_inc(dense_full[b], 1)

                def turn(part, stage, at, n, src):
                    b, d = begin(part, stage, n, at)
                    for t in PAIRS[n]:
                        for m in range(MC):
                            to = (t % 2) * 256 + m * 128
                            mm = pe.transpose(d[:, to:to + 128], src[:, t, m * 128:m * 128 + 128], ident[:, :])
                    mm.then_inc(dense_full[b], 1)

                def hn_to_channels(part, g, n):
                    pe.wait_ge(hn_ready, g * 4 + n + 1)
                    turn(part, "N", g, n, hn)

                def hn2_to_channels(part, g, at, n):
                    pe.wait_ge(hn2_ready, g * 4 + n + 1)
                    turn(part, "L", at, n, hn2)

                def queries_keys(part, g, n):
                    if n == 0:
                        wait_read(pe, part, "N", 3, g)
                    m, rest = divmod(n, 4)
                    of, u = divmod(rest, 2)
                    b, d = begin(part, "Q", n, g)
                    for k in range(MC):
                        at = k * 3 * C + of * C + m * 128
                        mm = product(d[:, 0:HALF], wqkv_h[:, at:at + 128], wqkv_l[:, at:at + 128],
                                     hnT_h[:, k, u * HALF:(u + 1) * HALF], hnT_l[:, k, u * HALF:(u + 1) * HALF],
                                     k == 0, k == MC - 1)
                    mm.then_inc(dense_full[b], 1)

                def values(part, g, n):
                    b, d = begin(part, "V", n, g)
                    for t in PAIRS[n]:
                        for k in range(MC):
                            at = k * 3 * C + 2 * C
                            mm = product(d[:, (t % 2) * 256:(t % 2) * 256 + 256],
                                         hnT_h[:, k, t * 128:t * 128 + 128], hnT_l[:, k, t * 128:t * 128 + 128],
                                         wqkv_h[:, at:at + C], wqkv_l[:, at:at + C], k == 0, k == MC - 1)
                    mm.then_inc(dense_full[b], 1)

                def scores(part, g, hc, hq):
                    if hq == 0:
                        wait_read(pe, part, "Q", 4 * hc + 3, g)
                    if hc > 0:
                        pe.wait_ge(scores_read, g * 8 + hq + 1)
                    settle(pe)
                    for t in range(TILES):
                        for b in range(4):
                            cols = slice(t * 128 + b * POS, t * 128 + b * POS + POS)
                            at = (hc * TILES + t) * POS
                            mm = pe.matmul(att[hq][b * 32:b * 32 + 32, at:at + POS],
                                           qT[hq * 32:hq * 32 + 32, hc, cols],
                                           kT[hq * 32:hq * 32 + 32, hc, cols], start=True, stop=True,
                                           tile_position=(hq * 32, b * 32))
                    mm.then_inc(scores_ready, 1)

                def attend(part, g, hc, b):
                    if b == 0:
                        wait_read(pe, part, "V", 3, g)
                        pe.wait_ge(pT_ready, g * 2 + hc + 1)
                    if hc == 0 and b == 0:
                        pe.wait_ge(scores_read, g * 8 + 8)
                    if hc == 0 and b == 3 and part != "zero":
                        pe.wait_ge(gshifted, g)
                    settle(pe)
                    for t in range(TILES):
                        for hq in range(HQ):
                            h = hc * HQ + hq
                            at = (hc * TILES + t) * POS
                            mm = pe.matmul(att[b][hq * 32:hq * 32 + 32, at:at + POS],
                                           v[b * 32:b * 32 + 32, t, h * DH:h * DH + DH],
                                           pT[b * 32:b * 32 + 32, h * TILES + t, :], start=True, stop=True,
                                           tile_position=(b * 32, hq * 32))
                    if hc == MC - 1:
                        mm.then_inc(attended, 1)

                def project(part, g, at, n):
                    if n == 0:
                        pe.wait_ge(oT_lo, g * 4 + 4)
                    b, d = begin(part, "O", n, at)
                    for t in PAIRS[n]:
                        for m in range(MC):
                            mm = product(d[:, (t % 2) * 256:(t % 2) * 256 + 256], oT_h[:, t, m, :], oT_l[:, t, m, :],
                                         wo_h[:, m * C:(m + 1) * C], wo_l[:, m * C:(m + 1) * C], m == 0, m == MC - 1)
                    mm.then_inc(dense_full[b], 1)

                def gates(part, g, at, n):
                    if n == 0:
                        if part != "end":
                            pe.wait_ge(scores_read, g * 8 + 16)
                        pe.matmul(att[3][:, 0:TILES * E], ones[:, :], view(bgs[:, 0, 0:1], [1, TILES * E]), start=True, stop=False)
                    wait_read(pe, part, "L", n, at)
                    for t in PAIRS[n]:
                        for m in range(MC):
                            mm = pe.matmul(att[3][:, t * E:(t + 1) * E], hn2T[:, m, t * 128:t * 128 + 128], wgs[:, m, :],
                                           start=False, stop=(t == TILES - 1 and m == MC - 1))
                    if n == 3:
                        mm.then_inc(gates_done, 1)

                def iteration(part, g):
                    for name, n in until(part, "Q", 4):
                        if name == "T":
                            transpose_patches(part, g + 1, g, [n])
                        elif name == "O":
                            project(part, g - 1, g, n)
                        elif name == "N":
                            hn_to_channels(part, g, n)
                        else:
                            queries_keys(part, g, n)
                    for n in range(4):
                        queries_keys(part, g, 4 + n)
                        scores(part, g, 0, n)
                    for n in range(4):
                        values(part, g, n)
                        scores(part, g, 1, n)
                    if part != "zero":
                        for n in range(4):
                            hn2_to_channels(part, g - 1, g, n)
                    for n in range(8):
                        if part != "last" and n < TILES:
                            embed(part, g + 1, g, n)
                        if part != "zero":
                            for pair in ((0,), (1,), (2, 3))[n] if n < 3 else ():
                                gates(part, g - 1, g, pair)
                        attend(part, g, n // 4, n % 4)

                pe.wait_ge(setup, 1)
                pe.wait_ge(ident_in, 16)
                transpose_patches("first", 0, 0, range(12))
                pe.wait_ge(weights_low, 1)
                for t in range(TILES):
                    embed("first", 0, 0, t)
                pe.wait_ge(weights_low, 3)
                pe.wait_ge(consts_in, 16 * 10)
                iteration("zero", 0)
                with pe.Fori(1, G - 1) as g:
                    iteration("loop", g)
                iteration("last", G - 1)
                for n in range(4):
                    project("end", G - 1, G - 1, n)
                for n in range(4):
                    hn2_to_channels("end", G - 1, G - 1, n)
                for n in range(4):
                    gates("end", G - 1, G - 1, n)

            @block.scalar
            def _(act):
                def full(part, stage, n, g):
                    b, turns = fill(part, stage, n, g)
                    act.wait_ge(dense_full[b], turns + 1)
                    return b, dense[b]

                def patches_high(part, p, at, ns):
                    for n in ns:
                        c, w0, nw = TSTEPS[n]
                        b, d = full(part, "T", n, at)
                        src, dst = patch_views(d, xT_h, c, w0, nw)
                        act.activation(dst, src, ACT.Copy).then_inc(xT_hi, 1)

                def normalise(n, g, src, dst, ready):
                    act.wait_ge(shift_ready[n], g + 1)
                    for t in range(TILES):
                        ins = act.activation(dst[:, t, :], src[:, t, :], ACT.Identity, scale=rstd[n][:, t:t + 1],
                                             bias=shift[n][:, t:t + 1])
                        if t % 2 or t == TILES - 1:
                            ins.then_inc(ready, 1)

                def hn_high(part, g, n):
                    b, d = full(part, "N", n, g)
                    src, dst = channel_views(d, hnT_h, PAIRS[n])
                    act.activation(dst, src, ACT.Copy).then_inc(hnT_hi, 1)

                def qk_out(part, g, ns):
                    for n in ns:
                        m, rest = divmod(n, 4)
                        of, u = divmod(rest, 2)
                        b, d = full(part, "Q", n, g)
                        act.activation((qT, kT)[of][:, m, u * HALF:(u + 1) * HALF], d[:, 0:HALF],
                                       ACT.Copy).then_inc(dense_free[b], 1)

                def v_out(part, g, ns):
                    for n in ns:
                        tiles = PAIRS[n]
                        b, d = full(part, "V", n, g)
                        act.activation(view(v[:, tiles[0], 0:1], [1, 256 * len(tiles)]), d[:, 0:256 * len(tiles)],
                                       ACT.Copy).then_inc(dense_free[b], 1)

                def softmax_exp(g, hc):
                    act.wait_ge(shifted, g * 2 + hc + 1)
                    w = view(win[:, hc, 0, 0, 0:1], [1, 2 * HIDX * 6])
                    act.activation(w, w, ACT.Exp, scale=SCALE).then_inc(exped, 1)

                def attended_high(g):
                    for n in range(4):
                        act.wait_ge(attended, g * 4 + n + 1)
                        src, dst = attended_views(att[n], oT_h, n)
                        act.activation(dst, src, ACT.Copy).then_inc(oT_hi, 1)

                def hn2_out(part, g, at):
                    act.wait_ge(hn2T_stored, g * 16 + 1)
                    for n, tiles in enumerate(PAIRS):
                        b, d = full(part, "L", n, at)
                        src, dst = channel_views(d, hn2T, tiles)
                        act.activation(dst, src, ACT.Copy).then_inc(dense_free[b], 1)

                def gate_exp(g):
                    act.wait_ge(gshifted, g + 1)
                    w = view(gate[:, 0, 0:1], [1, TILES * E])
                    act.activation(w, w, ACT.Exp).then_inc(gexped, 1)

                def iteration(part, g):
                    if part != "last":
                        patches_high(part, g + 1, g, range(3))
                    normalise(0, g, hpos, hn, hn_ready)
                    for name, n in until(part, "V", 0):
                        if name == "T" and n >= 3:
                            patches_high(part, g + 1, g, [n])
                        elif name == "N":
                            hn_high(part, g, n)
                        elif name == "Q":
                            qk_out(part, g, [n])
                    if part != "zero":
                        normalise(1, g - 1, h2, hn2, hn2_ready)
                    v_out(part, g, (0, 1))
                    softmax_exp(g, 0)
                    v_out(part, g, (2, 3))
                    if part != "zero":
                        hn2_out(part, g - 1, g)
                    softmax_exp(g, 1)
                    if part != "zero":
                        gate_exp(g - 1)
                    attended_high(g)

                for n, src in enumerate((w_patch, w_qkv, w_out)):
                    act.dma_start(WEIGHTS[n][2], src).then_inc(weight_in[n], 16)
                for dst, src in ((band[:, :], c_band), (window[:, :], c_window), (there[:, :], c_there),
                                 (windows[:, :], c_windows), (lower[:, :], c_lower), (same[:, :], c_same),
                                 (view(wgs[:, 0, 0:1], [1, MC * E]), w_gate),
                                 (b_embed[:, :], copies(b_patch, 128)), (view(six[:, 0, 0:1], [1, C]), copies(b_out, 128)),
                                 (view(bgs[:, 0, 0:1], [E, TILES], [1, E]), copies(b_gate, 1, TILES))):
                    act.dma_start(dst, src).then_inc(consts_in, 16)

                def weight_high(n):
                    hi, _, src = WEIGHTS[n]
                    act.wait_ge(weight_in[n], 16)
                    act.activation(hi[:, :], src, ACT.Copy).then_inc(weights_high, 1)

                weight_high(0)
                patches_high("first", 0, 0, range(12))
                weight_high(1)
                weight_high(2)
                iteration("zero", 0)
                with act.Fori(1, G - 1) as g:
                    iteration("loop", g)
                iteration("last", G - 1)
                normalise(1, G - 1, h2, hn2, hn2_ready)
                hn2_out("end", G - 1, G - 1)
                gate_exp(G - 1)

            @block.vector
            def _(dve):
                ln = [Steps(dve, ln_step[n], 2) for n in range(2)]
                soft = Steps(dve, soft_step, SOFT_STEPS)
                gs = Steps(dve, gate_step, 9)

                def full(part, stage, n, g):
                    b, turns = fill(part, stage, n, g)
                    dve.wait_ge(dense_full[b], turns + 1)
                    return b, dense[b]

                def patches_low(part, p, at, ns):
                    for n in ns:
                        c, w0, nw = TSTEPS[n]
                        dve.wait_ge(xT_hi, p * 12 + n + 1)
                        b, d = full(part, "T", n, at)
                        src, hi = patch_views(d, xT_h, c, w0, nw)
                        lo = patch_views(d, xT_l, c, w0, nw)[1]
                        dve.tensor_tensor(lo, src, hi.bitcast(F32), ALU.subtract).then_inc(dense_free[b], 1)

                def embed_out(part, p, at, ns):
                    if part != "first" and ns[0] == 0:
                        dve.wait_ge(h2_begun, p)
                    for n in ns:
                        tiles = PAIRS[n]
                        b, d = full(part, "E", n, at)
                        dve.tensor_tensor(view(hpos[:, tiles[0], 0:1], [C, len(tiles)], [1, C]),
                                          view(d[:, 0:1], [C, len(tiles)], [1, C]),
                                          view(b_embed[:, 0:1], [0, len(tiles)], [1, C]), ALU.add).then_inc(dense_free[b], 1)

                def statistics(n, g, src, tiles=range(TILES)):
                    s = ln[n]
                    s.group(g)
                    for t in tiles:
                        ins = dve.bn_stats(stat[n][:, t, :], src[:, t, :])
                    if TILES - 1 not in tiles:
                        return
                    s.did(ins)
                    s.wait()
                    settle(dve)
                    for t in range(TILES):
                        ins = dve.bn_aggr(mv[n][:, t, :], stat[n][:, t, :])
                    s.did(ins)
                    s.wait()
                    dve.tensor_scalar(negmean[n][:, :], mv[n][:, :, 0], -1.0, None, ALU.mult)
                    dve.tensor_scalar(vare[n][:, :], mv[n][:, :, 1], LN_EPS, None, ALU.add).then_inc(var_ready[n], 1)
                    s.end()

                def hn_low(part, g, n):
                    dve.wait_ge(hnT_hi, g * 4 + n + 1)
                    b, d = full(part, "N", n, g)
                    src, hi = channel_views(d, hnT_h, PAIRS[n])
                    lo = channel_views(d, hnT_l, PAIRS[n])[1]
                    dve.tensor_tensor(lo, src, hi.bitcast(F32), ALU.subtract).then_inc(dense_free[b], 1)

                def softmax_shift(g, hc):
                    s = soft
                    s.group(g * 2 + hc)
                    n = TILES
                    for hq in range(HQ):
                        dve.wait_ge(scores_ready, g * 8 + hc * 4 + hq + 1)
                        at = hc * HIDX + hq * n
                        ins = dve.tensor_tensor(banded[:, at:at + n, 0:POS],
                                                att[hq][:, hc * n * POS:(hc + 1) * n * POS].rearrange("p (k j) -> p k j", j=POS),
                                                view(band[:, 0:1], [0, n], [1, POS]), ALU.mult).then_inc(scores_read, 1)
                    dve.wait_ge(scores_read, g * 8 + hc * 4 + 4)
                    at = hc * HIDX
                    s.did(dve.tensor_reduce(six[:, at:at + HIDX, :], view(banded[:, at, 0:1], [BAND, HIDX], [1, 6], [6, BAND // 6]),
                                            AX.X, ALU.add))
                    s.wait()
                    for w in range(2):
                        ins = dve.tensor_tensor(win[:, hc, w], six[:, at:at + HIDX, :],
                                                view(window[:, 6 * w:6 * w + 1], [0, HIDX], [1, 6]), ALU.add)
                    s.did(ins)
                    s.wait()
                    flat = view(win[:, hc, 0, 0, 0:1], [6, 2 * HIDX], [1, 6])
                    s.did(dve.tensor_reduce(wstat[:, hc, :], flat, AX.X, ALU.max))
                    s.wait()
                    dve.tensor_tensor(flat, flat, view(wstat[:, hc, 0:1], [1, 2 * HIDX], [0, 6]), ALU.subtract).then_inc(shifted, 1)

                def softmax_weigh(g, hc):
                    s = soft
                    at = hc * HIDX
                    flat = view(win[:, hc, 0, 0, 0:1], [6, 2 * HIDX], [1, 6])
                    per = view(wstat[:, hc, 0:1], [1, 2 * HIDX], [0, 6])
                    dve.wait_ge(exped, g * 2 + hc + 1)
                    s.did(dve.tensor_reduce(wstat[:, hc, :], flat, AX.X, ALU.add))
                    s.wait()
                    s.did(dve.reciprocal(wstat[:, hc, :], wstat[:, hc, :]))
                    s.wait()
                    s.did(dve.tensor_tensor(wstat[:, hc, :], wstat[:, hc, :], there[:, :], ALU.mult))
                    s.wait()
                    s.did(dve.tensor_tensor(flat, flat, per, ALU.mult))
                    s.wait()
                    s.did(dve.tensor_tensor(prob[:, at:at + HIDX, :], win[:, hc, 0], win[:, hc, 1], ALU.add))
                    s.wait()
                    dve.tensor_tensor(view(banded[:, at, 0:1], [BAND, HIDX], [6, BAND // 6], [1, 6]),
                                      view(prob[:, at, 0:1], [6, HIDX], [0, BAND // 6], [1, 6]),
                                      view(band[:, 0:1], [0, HIDX], [6, BAND // 6], [1, 6]), ALU.mult).then_inc(spread_done, 1)
                    dve.wait_ge(spread_done, g * 2 + hc + 1)
                    dve.transpose(pT[:, at:at + HIDX, :], banded[:, at:at + HIDX, 0:POS]).then_inc(pT_ready, 1)
                    s.end()

                def attended_low(g, ns):
                    for n in ns:
                        dve.wait_ge(oT_hi, g * 4 + n + 1)
                        src, hi = attended_views(att[n], oT_h, n)
                        lo = attended_views(att[n], oT_l, n)[1]
                        dve.tensor_tensor(lo, src, hi.bitcast(F32), ALU.subtract).then_inc(oT_lo, 1)

                def residual(part, g, at, n):
                    if n == 0:
                        dve.wait_ge(h2_begun, g + 1)
                    b, d = full(part, "O", n, at)
                    w = [1, 256 * len(PAIRS[n])]
                    dve.tensor_tensor(view(h2[:, PAIRS[n][0], 0:1], w), d[:, 0:256 * len(PAIRS[n])],
                                      view(h2[:, PAIRS[n][0], 0:1], w), ALU.add).then_inc(dense_free[b], 1)

                def gates_shift(g):
                    s = gs
                    s.group(g)
                    dve.wait_ge(gates_done, g + 1)
                    logits = att[3][:, 0:TILES * E].rearrange("p (t e) -> p t e", e=E)
                    s.did(dve.tensor_reduce(gstat[:, 0:TILES], logits, AX.X, ALU.max))
                    s.wait()
                    dve.tensor_tensor(gate[:, :, :], logits, view(gstat[:, 0:1], [1, TILES], [0, E]), ALU.subtract).then_inc(gshifted, 1)

                def route_gates(g):
                    s = gs
                    dve.wait_ge(gexped, g + 1)
                    dve.wait_ge(scoresT_stored, g * 128 + 1)
                    s.did(dve.tensor_reduce(gstat[:, 0:TILES], gate[:, :, :], AX.X, ALU.add))
                    s.wait()
                    s.did(dve.reciprocal(gstat[:, TILES:2 * TILES], gstat[:, 0:TILES]))
                    s.wait()
                    s.did(dve.tensor_tensor(gate[:, :, :], gate[:, :, :], view(gstat[:, TILES:TILES + 1], [1, TILES], [0, E]), ALU.mult))
                    s.wait()
                    mine = view(gate[:, 0, 0:1], [E, TILES], [1, E], [0, E])
                    other = view(gate[:, 0, 0:1], [E, TILES], [0, E], [1, E])
                    dve.tensor_tensor(above[:, :, :, :], other, mine, ALU.is_gt)
                    s.did(dve.tensor_tensor(level[:, :, :, :], other, mine, ALU.is_equal))
                    s.wait()
                    flat = lambda a: view(a[:, 0, 0, 0:1], [E * E, TILES], [1, E * E])
                    s.did(dve.tensor_tensor(flat(level), flat(level), view(lower[:, 0:1], [0, TILES], [1, E * E]), ALU.mult))
                    s.wait()
                    s.did(dve.tensor_tensor(flat(above), flat(above), flat(level), ALU.add))
                    s.wait()
                    s.did(dve.tensor_reduce(rank[:, :, :], above[:, :, :, :], AX.X, ALU.add))
                    s.wait()
                    both = view(masked[:, 0:1], [1, TILES * E])
                    s.did(dve.scalar_tensor_tensor(both, view(rank[:, 0, 0:1], [1, TILES * E]), TOPK - 0.5,
                                                   view(gate[:, 0, 0:1], [1, TILES * E]), ALU.is_lt, ALU.mult))
                    s.wait()
                    dve.transpose(scoresT[:, :], masked[:, :]).then_inc(scoresT_ready, 1)
                    s.end()

                def weight_low(n):
                    hi, lo, src = WEIGHTS[n]
                    dve.wait_ge(weights_high, n + 1)
                    dve.tensor_tensor(lo[:, :], src, hi[:, :].bitcast(F32), ALU.subtract).then_inc(weights_low, 1)

                weight_low(0)
                patches_low("first", 0, 0, range(12))
                weight_low(1)
                weight_low(2)
                dve.wait_ge(setup, 1)
                dve.wait_ge(consts_in, 16 * 10)
                for t in range(TILES):
                    last = dve.tensor_scalar(b_attn[:, t, :], view(six[:, 0, 0:1], [1, C]), windows[:, t:t + 1], None, ALU.mult)
                last.then_inc(bias_spread, 1)
                embed_out("first", 0, 0, range(4))
                wait_read(dve, "first", "E", 3, 0)
                statistics(0, 0, hpos)

                def iteration(part, g):
                    for name, n in until(part, "Q", 4):
                        if name == "T":
                            patches_low(part, g + 1, g, [n])
                        elif name == "O":
                            residual(part, g - 1, g, n)
                        elif name == "N":
                            hn_low(part, g, n)
                    if part != "zero":
                        wait_read(dve, part, "O", 3, g)
                        statistics(1, g - 1, h2)
                    softmax_shift(g, 0)
                    softmax_weigh(g, 0)
                    softmax_shift(g, 1)
                    softmax_weigh(g, 1)
                    if part != "zero":
                        gates_shift(g - 1)
                        route_gates(g - 1)
                    if part != "last":
                        embed_out(part, g + 1, g, (0, 1))
                        wait_read(dve, part, "E", 1, g)
                        statistics(0, g + 1, hpos, range(0, 4))
                    attended_low(g, (0, 1))
                    if part != "last":
                        embed_out(part, g + 1, g, (2, 3))
                        wait_read(dve, part, "E", 3, g)
                        statistics(0, g + 1, hpos, range(4, TILES))
                    attended_low(g, (2, 3))

                iteration("zero", 0)
                with dve.Fori(1, G - 1) as g:
                    iteration("loop", g)
                iteration("last", G - 1)
                for n in range(4):
                    residual("end", G - 1, G - 1, n)
                wait_read(dve, "end", "O", 3, G - 1)
                statistics(1, G - 1, h2)
                gates_shift(G - 1)
                route_gates(G - 1)

        scores_in = [sem(f"scores_in{c}") for c in range(CH)]
        summed, route_step, loop_step, picked_ready, picked_stored = sem("summed"), sem("route_step"), sem("loop_step"), sem("picked_ready"), sem("picked_stored")
        ffn_in, zeroed = sem("ffn_in"), sem("zeroed")

        w_high, w_low = sem("w_high"), sem("w_low")
        t_in_loaded, t_high, t_low = sem("t_in_loaded"), sem("t_high"), sem("t_low")
        mask_loaded, mask_used = sem("mask_loaded"), sem("mask_used")
        spread_ready, b2_split = sem("spread_ready"), sem("b2_split")
        h_loaded, y_full, y_added, y_stored = sem("h_loaded"), sem("y_full"), sem("y_added"), sem("y_stored")
        hid_full, activated = sem("hid_full"), sem("activated")
        spread_full, mask_put = sem("spread_full"), sem("mask_put")
        hid_high, hid_low = sem("hid_high"), sem("hid_low")
        UT = TOK // 2
        STEPS3 = [(u, c) for u in range(2) for c in range(HID)]
        N3 = len(STEPS3)
        out_t = out.rearrange("(g t p) n -> g p t n", t=TILES, p=4 * Q)

        with nc.Block() as block:
            def rows(dram, c):
                return bass.AP(dram.tensor, dram.offset + c * CIMG * SEQ, [[SEQ, CIMG], [NTOK, E], [1, SEQ]])

            @block.sync
            def _(sp):
                def load_t(i):
                    sp.dma_start(view(t_in[:, 0, 0:1], [1, MC * GPOS]), h2n_d[i]).then_inc(t_in_loaded, 16)

                def load_mask(i):
                    for n in range(3):
                        sp.dma_start(mask16[n * GAP:n * GAP + E, :], mask_d[:, bass.ds(i * TOK, TOK)]).then_inc(mask_loaded, 16)

                def load_h(i):
                    sp.dma_start(h_in[:, :, :], out_t[i]).then_inc(h_loaded, 16)

                def store(i):
                    sp.wait_ge(y_added, i * 4 + 4)
                    sp.dma_start(out_t[i], y_out[:, :, :]).then_inc(y_stored, 16)

                sp.sem_inc(y_stored, 1)
                for c in range(CH):
                    sp.dma_start(route[:, c, 0:SEQ], rows(score_d, c)).then_inc(scores_in[c], 16)
                sp.dma_start(w1s[:, :], w1).then_inc(ffn_in, 16)
                load_t(0)
                for dst, src in ((b1s, b1), (w2s, w2), (spread32, c_spread)):
                    sp.dma_start(dst[:, :], src).then_inc(ffn_in, 16)
                sp.wait_ge(zeroed, 1)
                for n in range(3):
                    sp.dma_start(b2_left[n * GAP:n * GAP + E, :], b2).then_inc(ffn_in, 16)
                load_h(0)
                def masks(c):
                    sp.wait_ge(picked_ready, 1 + c * GPC)
                    sp.dma_start(rows(mask_d, c), picked[:, c, :]).then_inc(picked_stored, 16)
                    sp.wait_ge(picked_stored, c * 16 + 16)

                def step(i, last=False):
                    sp.wait_ge(t_low, i + 1)
                    load_t(i + 1)
                    if last:
                        masks((i + 1) // GPC)
                    sp.wait_ge(mask_put, i * N3 + N3)
                    sp.wait_ge(mask_used, i + 1)
                    load_mask(i + 1)
                    store(i)
                    load_h(i + 1)

                masks(0)
                load_mask(0)
                for c in range(CH):
                    with sp.Fori(c * GPC, c * GPC + GPC - 1) as i:
                        step(i)
                    if c < CH - 1:
                        step(c * GPC + GPC - 1, last=True)
                store(G - 1)
                sp.wait_ge(y_stored, G * 16 + 1)

            @block.tensor
            def _(pe):
                def product(o, a_h, a_l, b_h, b_l, start, stop):
                    pe.matmul(o, a_h, b_h, start=start, stop=False)
                    pe.matmul(o, a_l, b_h, start=False, stop=False)
                    return pe.matmul(o, a_h, b_l, start=False, stop=stop)

                def hidden(i, n):
                    u, c = STEPS3[n]
                    if n >= 2:
                        pe.wait_ge(activated, i * N3 + n - 1)
                    for k in range(MC):
                        at = k * E * SUB + c * 128
                        at_t = u * HALF + HALO
                        th, tl = (view(t[:, k, at_t:at_t + 1], [POS, BLOCKS // 2], [1, Q]) for t in (t_h, t_l))
                        mm = product(bank[n % 2][:, 0:UT], w1_h[:, at:at + 128], w1_l[:, at:at + 128], th, tl,
                                     k == 0, k == MC - 1)
                    mm.then_inc(hid_full, 1)

                def spread_mask(i, n):
                    u, c = STEPS3[n]
                    if n >= 2:
                        pe.wait_ge(mask_put, i * N3 + n - 1)
                    pe.matmul(bank[2 + n % 2][:, 0:UT], spread[:, c * 128:(c + 1) * 128],
                              mask16[0:E, u * UT:(u + 1) * UT], start=True, stop=True).then_inc(spread_full, 1)

                def outputs(i):
                    def place(t):
                        return bank[4 + t // 2][0:4 * Q, (t % 2) * 256:(t % 2) * 256 + 256], slice(t * 4 * Q, (t + 1) * 4 * Q)

                    pe.wait_ge(hid_low, i * N3 + HID)
                    for t in range(TILES):
                        o, cols = place(t)
                        mm = pe.matmul(o, mask16[:, cols], b2_parts[:, :], start=(t % 2 == 0), stop=False)
                    mm.then_inc(mask_used, 1)
                    for n, tiles in enumerate(PAIRS):
                        if n > 0:
                            pe.wait_ge(hid_low, i * N3 + N3)
                        for t in tiles:
                            o, cols = place(t)
                            for c in range(HID):
                                mm = product(o, hid_h[:, c, cols], hid_l[:, c, cols], w2_h[:, c * C:(c + 1) * C],
                                             w2_l[:, c * C:(c + 1) * C], False, c == HID - 1 and t == tiles[-1])
                        mm.then_inc(y_full, 1)

                for c in range(CH):
                    pe.wait_ge(scores_in[c], 16)
                    mm = pe.matmul(bank[7][:, 0:SEQ], same[:, :], route[:, c, 0:SEQ], start=(c == 0), stop=(c == CH - 1))
                mm.then_inc(summed, 1)
                pe.wait_ge(w_low, 1)
                pe.wait_ge(t_low, 1)
                for n in range(N3):
                    hidden(0, n)
                pe.wait_ge(spread_ready, 1)
                pe.wait_ge(mask_loaded, 48)
                for n in range(N3):
                    spread_mask(0, n)
                pe.wait_ge(w_low, 2)
                pe.wait_ge(b2_split, 5)
                outputs(0)
                with pe.Fori(1, G) as i:
                    pe.wait_ge(t_low, i + 1)
                    for n in range(N3):
                        hidden(i, n)
                        if n == 0:
                            pe.wait_ge(mask_loaded, i * 48 + 48)
                        spread_mask(i, n)
                    outputs(i)

            @block.scalar
            def _(act):
                def split_high(i):
                    act.wait_ge(t_in_loaded, i * 16 + 16)
                    act.activation(t_h[:, :, :], t_in[:, :, :], ACT.Copy).then_inc(t_high, 1)

                def high(i, n):
                    u, c = STEPS3[n]
                    act.wait_ge(mask_put, i * N3 + n + 1)
                    act.activation(hid_h[:, c, u * UT:(u + 1) * UT], hid[:, c, u * UT:(u + 1) * UT],
                                   ACT.Copy).then_inc(hid_high, 1)

                def gelu(i, n):
                    u, c = STEPS3[n]
                    act.wait_ge(hid_full, i * N3 + n + 1)
                    act.activation(hid[:, c, u * UT:(u + 1) * UT], bank[n % 2][:, 0:UT], ACT.Gelu,
                                   bias=b1s[:, c:c + 1]).then_inc(activated, 1)

                def group(i):
                    for n in range(N3):
                        gelu(i, n)
                        if n > 0:
                            high(i, n - 1)
                    high(i, N3 - 1)

                act.wait_ge(ffn_in, 16 * 7)
                act.activation(w1_h[:, :], w1s[:, :], ACT.Copy).then_inc(w_high, 1)
                split_high(0)
                act.activation(w2_h[:, :], w2s[:, :], ACT.Copy).then_inc(w_high, 1)
                act.activation(spread[:, :], spread32[:, :], ACT.Copy).then_inc(spread_ready, 1)
                for n in range(N3):
                    gelu(0, n)
                for n in range(N3):
                    high(0, n)
                split_high(1)
                with act.Fori(1, G - 1) as i:
                    group(i)
                    split_high(i + 1)
                group(G - 1)

            @block.vector
            def _(dve):
                def split_low(i):
                    dve.wait_ge(t_high, i + 1)
                    dve.tensor_tensor(t_l[:, :, :], t_in[:, :, :], t_h[:, :, :].bitcast(F32), ALU.subtract).then_inc(t_low, 1)

                def low(i, n):
                    u, c = STEPS3[n]
                    cols = slice(u * UT, (u + 1) * UT)
                    dve.wait_ge(hid_high, i * N3 + n + 1)
                    dve.tensor_tensor(hid_l[:, c, cols], hid[:, c, cols], hid_h[:, c, cols].bitcast(F32),
                                      ALU.subtract).then_inc(hid_low, 1)

                def group(i):
                    for n, (u, c) in enumerate(STEPS3):
                        cols = slice(u * UT, (u + 1) * UT)
                        dve.wait_ge(activated, i * N3 + n + 1)
                        dve.wait_ge(spread_full, i * N3 + n + 1)
                        dve.tensor_tensor(hid[:, c, cols], bank[2 + n % 2][:, 0:UT], hid[:, c, cols],
                                          ALU.mult).then_inc(mask_put, 1)
                        if n > 0:
                            low(i, n - 1)
                    low(i, N3 - 1)

                def add(i):
                    dve.wait_ge(h_loaded, i * 16 + 16)
                    dve.wait_ge(y_stored, i * 16 + 1)
                    for n, tiles in enumerate(PAIRS):
                        dve.wait_ge(y_full, i * 4 + n + 1)
                        w = [1, 256 * len(tiles)]
                        dve.tensor_tensor(view(y_out[:, tiles[0], 0:1], w), bank[4 + n][0:4 * Q, 0:256 * len(tiles)],
                                          view(h_in[:, tiles[0], 0:1], w), ALU.add).then_inc(y_added, 1)

                def split_bias():
                    dve.wait_ge(ffn_in, 16 * 7)
                    dve.tensor_copy(b2_parts[:, :], b2_left[:, :]).then_inc(b2_split, 1)
                    dve.wait_ge(b2_split, 1)
                    for at in (GAP, 2 * GAP):
                        last = dve.tensor_tensor(b2_left[at:at + GAP, :], b2_left[at:at + GAP, :], b2_parts[at:at + GAP, :], ALU.subtract)
                    last.then_inc(b2_split, 1)
                    dve.wait_ge(b2_split, 2)
                    for at in (GAP, 2 * GAP):
                        last = dve.tensor_copy(b2_parts[at:at + GAP, :], b2_left[at:at + GAP, :])
                    last.then_inc(b2_split, 1)
                    dve.wait_ge(b2_split, 3)
                    third = slice(2 * GAP, 3 * GAP)
                    dve.tensor_tensor(b2_left[third, :], b2_left[third, :], b2_parts[third, :], ALU.subtract).then_inc(b2_split, 1)
                    dve.wait_ge(b2_split, 4)
                    dve.tensor_copy(b2_parts[third, :], b2_left[third, :]).then_inc(b2_split, 1)

                def pick(s, c):
                    s.did(dve.max(best[:, c, :], route[:, c, :]))
                    s.wait()
                    settle(dve)
                    s.did(dve.match_replace(route[:, c, :], best[:, c, :], route[:, c, :], -1.0))
                    s.wait()
                    settle(dve)

                def show_picked(c):
                    dve.tensor_scalar(picked[:, c, :], route[:, c, 0:SEQ], 0.0, None, ALU.is_lt).then_inc(picked_ready, 1)

                def weigh(s, c):
                    s.did(dve.scalar_tensor_tensor(route[:, c, 0:SEQ], route[:, c, 0:SEQ], float(B), rden[:, :], ALU.mult, ALU.mult))
                    s.wait()

                def rank_first():
                    s = Steps(dve, route_step, 3 + CH + 2 * ROUNDS)
                    s.group(0)
                    first = ROUNDS * 8 - PICK
                    dve.memset(route[:, 0, SEQ:SEQ + first], BIG)
                    last = dve.memset(route[:, 0, SEQ + first:SEQ + PAD], -1.0)
                    if CH > 1:
                        last = dve.memset(route[:, 1:, SEQ:SEQ + PAD], BIG)
                    s.did(last)
                    dve.wait_ge(summed, 1)
                    s.did(dve.tensor_scalar(rden[:, :], bank[7][:, 0:SEQ], GATE_EPS, None, ALU.add))
                    s.wait()
                    s.did(dve.reciprocal(rden[:, :], rden[:, :]))
                    s.wait()
                    weigh(s, 0)
                    for _ in range(ROUNDS):
                        pick(s, 0)
                    show_picked(0)
                    for c in range(1, CH):
                        weigh(s, c)
                    s.end()

                loop = Steps(dve, loop_step, 2 * LOOP_ROUNDS // GPC)

                def step(i, c):
                    group(i)
                    if c < CH:
                        loop.group(i)
                        for _ in range(LOOP_ROUNDS // GPC):
                            pick(loop, c)
                        show_picked(c)
                        loop.end()
                    split_low(i + 1)
                    add(i)

                rank_first()
                split_bias()
                step(0, 1)
                for c in range(1, CH + 1):
                    with dve.Fori(max(1, (c - 1) * GPC), min(c * GPC, G - 1)) as i:
                        step(i, c)
                group(G - 1)
                add(G - 1)

            @block.gpsimd
            def _(pool):
                pool.memset(b2_left[:, :], 0.0)
                pool.memset(mask16[:, :], 0.0).then_inc(zeroed, 1)
                pool.wait_ge(w_high, 1)
                pool.tensor_tensor(w1_l[:, :], w1s[:, :], w1_h[:, :].bitcast(F32), ALU.subtract).then_inc(w_low, 1)
                pool.wait_ge(t_high, 1)
                pool.tensor_tensor(t_l[:, :, :], t_in[:, :, :], t_h[:, :, :].bitcast(F32), ALU.subtract).then_inc(t_low, 1)
                pool.wait_ge(w_high, 2)
                pool.tensor_tensor(w2_l[:, :], w2s[:, :], w2_h[:, :].bitcast(F32), ALU.subtract).then_inc(w_low, 1)


_OUT = "out_dram"


def kernel(x, L0_tok_W, L0_tok_b, L0_attn_w_qkv, L0_attn_w_out, L0_attn_b_out, L0_ffn_w_gate_w, L0_ffn_w_gate_b,
           L0_ffn_W1, L0_ffn_b1, L0_ffn_W2, L0_ffn_b2):
    import numpy as np
    import concourse.bacc as bacc
    from concourse.bass_utils import run_bass_kernel_spmd

    def chunks(a):
        a = np.asarray(a)
        return a.reshape(-1, 128, a.shape[1]).transpose(1, 0, 2).reshape(128, -1)

    arrays = {
        "x": x, "w_patch": chunks(np.asarray(L0_tok_W).T), "b_patch": np.asarray(L0_tok_b).reshape(1, C),
        "w_qkv": chunks(L0_attn_w_qkv), "w_out": chunks(L0_attn_w_out), "b_out": np.asarray(L0_attn_b_out).reshape(1, C),
        "w_gate": chunks(L0_ffn_w_gate_w), "b_gate": np.asarray(L0_ffn_w_gate_b).reshape(1, E),
        "w1": chunks(np.asarray(L0_ffn_W1).transpose(1, 0, 2).reshape(C, E * SUB)),
        "b1": np.asarray(L0_ffn_b1).reshape(HID, 128).T,
        "w2": chunks(np.asarray(L0_ffn_W2).reshape(E * SUB, C)), "b2": np.asarray(L0_ffn_b2),
    }
    arrays.update(shape_constants(np))
    arrays = {name: np.ascontiguousarray(a) for name, a in arrays.items()}
    B = arrays["x"].shape[0]
    nc = bacc.Bacc("TRN2", target_bir_lowering=False, num_devices=1)
    args = [nc.dram_tensor(f"in_{name}", a.shape, mybir.dt.from_np(a.dtype), kind="ExternalInput").ap()
            for name, a in arrays.items()]
    args.append(nc.dram_tensor(_OUT, (B * SEQ, C), F32, kind="ExternalOutput").ap())
    vit_layer(nc, *args)
    r = run_bass_kernel_spmd(nc, [{f"in_{name}": a for name, a in arrays.items()}], core_ids=[0])
    return r.results[0][_OUT].reshape(B, SEQ, C)
```

```python
from contextlib import ExitStack

import concourse.bass as bass
from concourse import mybir

F32 = mybir.dt.float32
F32R = mybir.dt.float32r
BF16 = mybir.dt.bfloat16
ALU = mybir.AluOpType
ACT = mybir.ActivationFunctionType
AX = mybir.AxisListType

C = 256
MC = C // 128
PATCH = 16
SIDE = 14
SEQ = SIDE * SIDE
IMG = 4
ROWS = IMG * SIDE
TOK = IMG * SEQ
HEADS, DH, KS, STRIDE = 8, 32, 4, 2
HALO = STRIDE
POS = 32
Q = POS - 2 * HALO
OWN = 4 * Q
BLOCKS = TOK // Q
TILES = BLOCKS // 4
GPOS = BLOCKS * POS
HALF = GPOS // 2
UT = TOK // 2
BAND = 36
HQ = 4
HIDX = HQ * TILES
IDX = MC * HIDX
E, SUB, TOPK = 8, 64, 2
HID = E * SUB // 128
KC = 3 * PATCH * PATCH // 128
LN_EPS = 1e-5
GATE_EPS = 1e-6
SCALE = float(C) ** -0.5
PICK = SEQ // 2
GAP = 32
ROUNDS = -(-PICK // 8)
GPC = 128 // E // IMG
LOOP_ROUNDS = -(-ROUNDS // GPC) * GPC
PAD = LOOP_ROUNDS * 8 - PICK
BIG = 1e30


def shape_constants(np):
    pos = np.arange(128)
    i = pos % POS
    pair = i // 2
    kap = np.arange(BAND)
    band = ((np.abs(kap[None, :] // 2 - pair[:, None]) <= 1) & (kap[None, :] < POS)).astype(np.float32)
    slot = (np.arange(6) // 2)[None, :]
    out0 = (pair[:, None] + 1) % 3 == slot
    out1 = (pair[:, None] - 1) % 3 == slot
    window = np.stack([np.where(out0, -BIG, 0), np.where(out1, -BIG, 0)], 1).astype(np.float32)
    block = (np.arange(TILES)[None, :] * 4 + (pos // POS)[:, None]) % (SEQ // Q)
    has0 = ~((block == 0) & (pair[:, None] == 1))
    has1 = ~((block == SEQ // Q - 1) & (pair[:, None] == POS // 2 - 2))
    has = np.stack([has0, has1], 1).astype(np.float32)
    there = np.broadcast_to(has[:, :, None, :], (128, 2, HQ, TILES)).reshape(128, 2 * HIDX)
    windows = has.sum(1)
    e = np.arange(E)
    lower = np.broadcast_to((e[None, :] < e[:, None]).reshape(1, E * E), (128, E * E))
    same = (pos[:, None] % E == pos[None, :] % E)
    f = lambda a: np.ascontiguousarray(a, dtype=np.float32)
    order = np.argsort((i < HALO) | (i >= POS - HALO), kind="stable")
    return {"c_ident": f(np.eye(128)), "c_own_first": f(np.eye(128)[:, order]), "c_band": f(band), "c_window": f(window.reshape(128, 12)),
            "c_there": f(there), "c_windows": f(windows), "c_lower": f(lower), "c_same": f(same)}


class Steps:

    def __init__(self, eng, sem, per_group):
        self.eng, self.sem, self.per_group = eng, sem, per_group

    def group(self, g):
        self.base, self.n = g * self.per_group, 0

    def did(self, ins):
        ins.then_inc(self.sem, 1)
        self.n += 1

    def wait(self):
        self.eng.wait_ge(self.sem, self.base + self.n)

    def end(self):
        assert self.n == self.per_group, self.n


def vit_layer(nc, x, w_patch, b_patch, w_qkv, w_out, b_out, w_gate, b_gate, w1, b1, w2, b2,
              c_ident, c_own_first, c_band, c_window, c_there, c_windows, c_lower, c_same, out):
    B = x.shape[0]
    G = B // IMG
    NTOK = B * SEQ
    CH = B * E // 128
    CIMG = 128 // E

    h2n_d = nc.dram_tensor("normalised_tokens", (G, 128, MC * TOK), F32, kind="Internal").ap()
    score_d = nc.dram_tensor("gate_scores", (E, NTOK), F32, kind="Internal").ap()
    mask_d = nc.dram_tensor("picked", (E, NTOK), BF16, kind="Internal").ap()

    def view(ap, *dims):
        return bass.AP(ap.tensor, ap.offset, [list(ap.ap[0])] + [list(d) for d in dims])

    weights = ExitStack()
    with weights:
        def tensor(stack, name, shape, dt=F32):
            return stack.enter_context(nc.sbuf_tensor(name, shape, dt))

        def sem(name):
            return weights.enter_context(nc.semaphore(name))

        bank = [weights.enter_context(nc.psum_tensor(f"bank{n}", [128, 512], F32)) for n in range(8)]
        att, dense = bank[:4], bank[4:]

        ident = tensor(weights, "ident", [128, 128])
        own_first = tensor(weights, "own_first", [128, 128])
        same = tensor(weights, "same", [128, 128])
        b1s = tensor(weights, "b1s", [128, HID])
        b2_left = tensor(weights, "b2_left", [3 * GAP, C])
        b2_parts = tensor(weights, "b2_parts", [3 * GAP, C], BF16)

        one = ExitStack()
        band = tensor(one, "band", [128, BAND])
        window = tensor(one, "window", [128, 12])
        there = tensor(one, "there", [128, 2 * HIDX])
        windows = tensor(one, "windows", [128, TILES])
        lower = tensor(one, "lower", [128, E * E])
        b_embed = tensor(one, "b_embed", [128, C])
        b_attn = tensor(one, "b_attn", [128, TILES, C])
        wgs = tensor(one, "wgs", [128, MC, E])
        bgs = tensor(one, "bgs", [1, TILES, E])
        ones = tensor(one, "ones", [1, 128])
        eps = tensor(one, "eps", [128, 2 * TILES])
        wp_h = tensor(one, "wp_h", [128, KC * C], F32R)
        wp_l = tensor(one, "wp_l", [128, KC * C], F32R)
        wqkv_h = tensor(one, "wqkv_h", [128, MC * 3 * C], F32R)
        wqkv_l = tensor(one, "wqkv_l", [128, MC * 3 * C], F32R)
        wo_h = tensor(one, "wo_h", [128, MC * C], F32R)
        wo_l = tensor(one, "wo_l", [128, MC * C], F32R)
        raw = tensor(one, "raw", [2 * ROWS, 8 * SIDE * PATCH])
        patches = tensor(one, "patches", [2 * ROWS, 3, SIDE, 128])
        xT_h = tensor(one, "xT_h", [128, KC, GPOS], F32R)
        xT_l = tensor(one, "xT_l", [128, KC, GPOS], F32R)
        hpos = tensor(one, "hpos", [128, TILES, C])
        hn = tensor(one, "hn", [128, TILES, C])
        hnT_h = tensor(one, "hnT_h", [128, MC, GPOS], F32R)
        hnT_l = tensor(one, "hnT_l", [128, MC, GPOS], F32R)
        qT = tensor(one, "qT", [128, MC, GPOS])
        kT = tensor(one, "kT", [128, MC, GPOS])
        v = tensor(one, "v", [128, TILES, C])
        banded = tensor(one, "banded", [128, IDX, BAND])
        six = tensor(one, "six", [128, IDX, 6])
        win = tensor(one, "win", [128, MC, 2, HIDX, 6])
        wstat = tensor(one, "wstat", [128, MC, 2 * HIDX])
        prob = tensor(one, "prob", [128, IDX, 6])
        oT_h = tensor(one, "oT_h", [128, TILES, MC, 128], F32R)
        oT_l = tensor(one, "oT_l", [128, TILES, MC, 128], F32R)
        h2 = tensor(one, "h2", [128, TILES, C])
        hn2 = hn
        hn2T = tensor(one, "hn2T", [128, MC, TOK])
        stat = [tensor(one, f"stat{n}", [128, TILES, 6]) for n in range(2)]
        mv = [tensor(one, f"mv{n}", [128, TILES, 2]) for n in range(2)]
        vare = [tensor(one, f"vare{n}", [128, TILES]) for n in range(2)]
        rstd = [tensor(one, f"rstd{n}", [128, TILES]) for n in range(2)]
        negmean = [tensor(one, f"negmean{n}", [128, TILES]) for n in range(2)]
        shift = [tensor(one, f"shift{n}", [128, TILES]) for n in range(2)]
        gate = tensor(one, "gate", [OWN, TILES, E])
        gstat = tensor(one, "gstat", [OWN, 2 * TILES])
        above = view(win[0:OWN, 0, 0, 0, 0:1], [E * E, TILES], [E, E], [1, E])
        level = tensor(one, "level", [OWN, TILES, E, E])
        rank = tensor(one, "rank", [OWN, TILES, E])
        masked = tensor(one, "masked", [128, 64])
        scoresT = tensor(one, "scoresT", [128, 64])
        pT = qT[:, :, :].rearrange("p m n -> p (m n)").rearrange("p (k j) -> p k j", j=POS)
        one.close()

        route = tensor(weights, "route", [128, CH, SEQ + PAD])
        rden = tensor(weights, "rden", [128, SEQ])
        best = tensor(weights, "best", [128, CH, 8])
        picked = tensor(weights, "picked_sb", [128, CH, SEQ], BF16)

        three = ExitStack()
        w1s = tensor(three, "w1s", [128, MC * E * SUB])
        w2s = tensor(three, "w2s", [128, HID * C])
        w1_h = tensor(three, "w1_h", [128, MC * E * SUB], F32R)
        w1_l = tensor(three, "w1_l", [128, MC * E * SUB], F32R)
        w2_h = tensor(three, "w2_h", [128, HID * C], F32R)
        w2_l = tensor(three, "w2_l", [128, HID * C], F32R)
        t_in = tensor(three, "t_in", [128, MC, TOK])
        t_h = tensor(three, "t_h", [128, MC, TOK], F32R)
        t_l = tensor(three, "t_l", [128, MC, TOK], F32R)
        h_in = tensor(three, "h_in", [OWN, TILES, C])
        y_out = tensor(three, "y_out", [OWN, TILES, C])
        mask16 = tensor(three, "mask16", [3 * GAP, TOK], BF16)
        unit_mask = tensor(three, "unit_mask", [128, HID, TOK], BF16)
        hid = tensor(three, "hid", [128, HID, TOK])
        hid_h = tensor(three, "hid_h", [128, HID, TOK], F32R)
        hid_l = tensor(three, "hid_l", [128, HID, TOK], F32R)
        three.close()

        def stage(name, *ns):
            return [(name, n) for n in ns]

        T, Q8 = stage("T", *range(12)), stage("Q", *range(8))
        four = {name: stage(name, *range(4)) for name in "NVELO"}
        O4 = four["O"]
        BEGIN = four["N"] + T[4:7] + [fill for pair in zip(Q8[0:4], T[7:11]) for fill in pair] + T[11:] + Q8[4:8] + four["V"]
        FILLS = {"first": T,
                 "zero": T[0:4] + BEGIN + four["E"],
                 "loop": T[0:3] + O4[0:2] + T[3:4] + O4[2:4] + BEGIN + four["L"] + four["E"],
                 "last": O4 + four["N"] + Q8 + four["V"] + four["L"],
                 "end": O4 + four["L"]}

        def until(part, name, n):
            return FILLS[part][:FILLS[part].index((name, n))]

        TURNS = {part: len(fills) // 4 for part, fills in FILLS.items()}
        BEFORE = {"first": 0, "zero": TURNS["first"], "loop": TURNS["first"] + TURNS["zero"]}
        BEFORE["last"] = BEFORE["loop"] + (G - 2) * TURNS["loop"]
        BEFORE["end"] = BEFORE["last"] + TURNS["last"]

        def fill(part, stage, n, g):
            at = FILLS[part].index((stage, n))
            turns = BEFORE[part] + at // 4
            if part == "loop":
                turns = g * TURNS["loop"] + (turns - TURNS["loop"])
            return at % 4, turns

        def wait_read(eng, part, stage, n, g):
            b, turns = fill(part, stage, n, g)
            eng.wait_ge(dense_free[b], turns + 1)

        PAIRS = [(0, 1), (2, 3), (4, 5), (6,)]
        TSTEPS = [(c, w, min(4, SIDE - w)) for c in range(3) for w in range(0, SIDE, 4)]
        assert len(TSTEPS) == 12 and len(PAIRS) == 4
        SOFT_STEPS = 8

        dense_full = [sem(f"dense_full{b}") for b in range(4)]
        dense_free = [sem(f"dense_free{b}") for b in range(4)]
        consts_in = sem("consts_in")
        ident_in = sem("ident_in")
        weight_in = [sem(f"weight_in{n}") for n in range(3)]
        weights_high, weights_low = sem("weights_high"), sem("weights_low")
        setup = sem("setup")
        raw_loaded, patched = [sem(f"raw_loaded{c}") for c in range(3)], sem("patched")
        xT_hi = sem("xT_hi")
        halo_copied = sem("halo_copied")
        first_halo, first_embedded, first_read = sem("first_halo"), sem("first_embedded"), sem("first_read")
        keys_whole = sem("keys_whole")
        h2_begun = sem("h2_begun")
        bias_spread = sem("bias_spread")
        var_ready = [sem(f"var_ready{n}") for n in range(2)]
        rstd_ready = [sem(f"rstd_ready{n}") for n in range(2)]
        shift_ready = [sem(f"shift_ready{n}") for n in range(2)]
        hn_ready = sem("hn_ready")
        hnT_hi = sem("hnT_hi")
        scores_ready, scores_read = sem("scores_ready"), sem("scores_read")
        shifted, exped = sem("shifted"), sem("exped")
        spread_done, pT_ready = sem("spread_done"), sem("pT_ready")
        attended = sem("attended")
        oT_hi, oT_lo = sem("oT_hi"), sem("oT_lo")
        h2_stored = sem("h2_stored")
        hn2_ready = sem("hn2_ready")
        hn2T_stored = sem("hn2T_stored")
        gates_done = sem("gates_done")
        gshifted, gexped = sem("gshifted"), sem("gexped")
        scoresT_ready, scoresT_stored = sem("scoresT_ready"), sem("scoresT_stored")
        ln_step = [sem(f"ln_step{n}") for n in range(2)]
        soft_step, gate_step = sem("soft_step"), sem("gate_step")

        passed = sem("passed")

        def settle(eng):
            eng.sem_inc(passed, 1)

        def patch_views(d, xt, c, w0, nw):
            src = view(d[:, 0:1], [2, 2 * BLOCKS], [1, 2], [2 * ROWS, nw])
            dst = view(xt[:, 2 * c, HALO + w0:HALO + w0 + 1], [POS, 2 * BLOCKS], [SIDE, 2], [1, nw])
            return src, dst

        def own(a, u):
            at = u * HALF + HALO
            return view(a[:, at:at + 1], [POS, BLOCKS // 2], [1, Q])

        def attended_views(bank, o, n):
            src = bank[:, 0:MC * TILES * POS].rearrange("p (m t i) -> p m t i", m=MC, i=POS)
            dst = view(o[:, 0, 0, n * POS:n * POS + 1], [128, MC], [MC * 128, TILES], [1, POS])
            return src, dst

        def channel_views(d, a, tiles, columns=128):
            src = d[:, 0:256 * len(tiles)].rearrange("p (t m c) -> p m t c", m=MC, c=128)[:, :, :, 0:columns]
            dst = a[:, :, tiles[0] * columns:(tiles[-1] + 1) * columns].rearrange("p m (t c) -> p m t c", c=columns)
            return src, dst

        x_v = x.rearrange("(g b) c (n f r) w -> g f c b n (r w)", b=IMG, n=SIDE, f=2)
        out_v = out.rearrange("(g t b i) n -> g b i t n", t=TILES, b=4, i=Q)

        with nc.Block() as block:
            def copies(row, *counts):
                return bass.AP(row.tensor, row.offset, [[0, n] for n in counts] + [[1, row.shape[-1]]])

            WEIGHTS = ((wp_h, wp_l, view(hpos[:, 0, 0:1], [1, KC * C])),
                       (wqkv_h, wqkv_l, view(hn2T[:, 0, 0:1], [1, MC * 3 * C])),
                       (wo_h, wo_l, view(hn[:, 0, 0:1], [1, MC * C])))
            FIRST_RAW = (raw, *(view(a[:, 0, 0:1], [1, 8 * SIDE * PATCH])[0:2 * ROWS] for a in (h2, v)))

            @block.sync
            def _(sp):
                def load(p, part=None):
                    for c in range(3):
                        to = FIRST_RAW[c] if part == "first" else raw
                        if part == "second" and c == 0:
                            sp.wait_ge(patched, 1)
                        elif part != "first":
                            sp.wait_ge(patched, p * 3 + c)
                        for f in range(2):
                            sp.dma_start(to[f * ROWS:(f + 1) * ROWS, :], x_v[p, f, c]).then_inc(raw_loaded[c], 16)

                def store_h2(part, g, at):
                    wait_read(sp, part, "O", 3, at)
                    for b in range(4):
                        sp.dma_start(out_v[g, b], h2[b * POS + HALO:b * POS + HALO + Q, :, :]).then_inc(h2_stored, 16)

                def store_rest(part, g, at):
                    wait_read(sp, part, "L", 3, at)
                    sp.dma_start(h2n_d[g], view(hn2T[:, 0, 0:1], [1, MC * TOK])).then_inc(hn2T_stored, 16)
                    sp.wait_ge(scoresT_ready, g + 1)
                    for b in range(4):
                        for half in range(2):
                            tiles = min(4, TILES - 4 * half)
                            at = g * TOK + half * 4 * OWN + b * 32
                            n = min(32, OWN - b * 32)
                            dst = bass.AP(score_d.tensor, score_d.offset + at, [[OWN, tiles], [NTOK, E], [1, n]])
                            src = scoresT[b * 32:b * 32 + tiles * E, half * 32:half * 32 + n]
                            sp.dma_start(dst, src).then_inc(scoresT_stored, 16)

                sp.dma_start(ident[:, :], c_ident).then_inc(ident_in, 16)
                load(0, "first")
                for stored in (h2_stored, hn2T_stored, scoresT_stored):
                    sp.sem_inc(stored, 1)
                load(1, "second")
                load(2)
                with sp.Fori(1, G - 2) as g:
                    load(g + 2)
                    store_h2("loop", g - 1, g)
                    store_rest("loop", g - 1, g)
                store_h2("loop", G - 3, G - 2)
                store_rest("loop", G - 3, G - 2)
                store_h2("last", G - 2, G - 1)
                store_rest("last", G - 2, G - 1)
                store_h2("end", G - 1, G - 1)
                store_rest("end", G - 1, G - 1)
                sp.wait_ge(h2_stored, G * 64 + 1)
                sp.wait_ge(hn2T_stored, G * 16 + 1)
                sp.wait_ge(scoresT_stored, G * 128 + 1)

            @block.gpsimd
            def _(pool):
                pool.memset(ones[:, :], 1.0)
                pool.memset(eps[:, :], -0.5)
                pool.memset(masked[:, :], 0.0)
                pool.memset(banded[:, :, POS:BAND], 0.0)
                pool.memset(view(qT[:, 0, 0:1], [1, MC * GPOS]), 0.0)
                pool.memset(kT[:, :, 0:HALO], 0.0)
                pool.memset(kT[:, :, GPOS - HALO:GPOS], 0.0)
                for xt in (xT_h, xT_l):
                    for k in range(0, KC, 2):
                        pool.memset(xt[:, k, 0:HALO].bitcast(F32), 0.0)
                        last = pool.memset(xt[:, k + 1, GPOS - HALO:GPOS].bitcast(F32), 0.0)
                last.then_inc(setup, 1)
                pool.wait_ge(setup, 1)

                def root(n, g):
                    pool.wait_ge(var_ready[n], g + 1)
                    pool.tensor_tensor(rstd[n][:, :], vare[n][:, :], eps[:, 0:TILES], ALU.pow).then_inc(rstd_ready[n], 1)
                    pool.wait_ge(rstd_ready[n], g + 1)
                    pool.tensor_tensor(shift[n][:, :], negmean[n][:, :], rstd[n][:, :], ALU.mult).then_inc(shift_ready[n], 1)

                def begin_h2(g):
                    if not isinstance(g, int) or g > 0:
                        pool.wait_ge(h2_stored, g * 64 + 1)
                        pool.wait_ge(hn2_ready, g * 4)
                        settle(pool)
                    else:
                        pool.wait_ge(bias_spread, 1)
                    pool.tensor_tensor(view(h2[:, 0, 0:1], [1, TILES * C]), view(hpos[:, 0, 0:1], [1, TILES * C]),
                                       view(b_attn[:, 0, 0:1], [1, TILES * C]), ALU.add).then_inc(h2_begun, 1)

                def halo(part, at, c=None):
                    wait_read(pool, part, "T", 11 if c is None else 4 * c + 3, at)
                    settle(pool)
                    k0, n = (0, KC * BLOCKS - 1) if c is None else (2 * c, 2 * BLOCKS - 1)
                    for xt in (xT_h, xT_l):
                        for to, of in ((POS, Q), (Q + HALO, POS + HALO)):
                            ins = pool.tensor_scalar(view(xt[:, k0, to:to + 1], [POS, n], [1, HALO]),
                                                     view(xt[:, k0, of:of + 1], [POS, n], [1, HALO]).bitcast(F32),
                                                     1.0, 0.0, ALU.mult, ALU.add)
                    ins.then_inc(halo_copied if c is None else first_halo, 1)

                def gather_patches(p, c, part, at):
                    pool.wait_ge(raw_loaded[c], p * 32 + 32)
                    if part is not None:
                        b, turns = fill(part, "T", 4 * c + 3, at)
                        pool.wait_ge(dense_full[b], turns + 1)
                    settle(pool)
                    pool.tensor_scalar(patches[:, c, :, :].rearrange("p w (r i) -> p r w i", i=PATCH),
                                       (raw if part is not None else FIRST_RAW[c])[:, :].rearrange("p (r w i) -> p r w i", r=8, i=PATCH),
                                       1.0, 0.0, ALU.mult, ALU.add).then_inc(patched, 1)

                def iteration(part, g, gathers=True):
                    if gathers:
                        gather_patches(g + 2, 0, part, g)
                        gather_patches(g + 2, 1, part, g)
                    halo(part, g)
                    if part != "zero":
                        root(1, g - 1)
                    if gathers:
                        gather_patches(g + 2, 2, part, g)
                    begin_h2(g)
                    root(0, g + 1)

                gather_patches(0, 0, None, 0)
                gather_patches(0, 1, None, 0)
                halo("first", 0, 0)
                gather_patches(0, 2, None, 0)
                halo("first", 0, 1)
                halo("first", 0, 2)
                gather_patches(1, 0, "first", 0)
                root(0, 0)
                gather_patches(1, 1, "first", 0)
                gather_patches(1, 2, "first", 0)
                iteration("zero", 0)
                with pool.Fori(1, G - 2) as g:
                    iteration("loop", g)
                iteration("loop", G - 2, gathers=False)
                root(1, G - 2)
                begin_h2(G - 1)
                root(1, G - 1)

            @block.tensor
            def _(pe):
                def begin(part, stage, n, g):
                    b, turns = fill(part, stage, n, g)
                    if not isinstance(turns, int) or turns > 0:
                        pe.wait_ge(dense_free[b], turns)
                    return b, dense[b]

                def product(o, a_h, a_l, b_h, b_l, start, stop):
                    pe.matmul(o, a_h, b_h, start=start, stop=False)
                    pe.matmul(o, a_l, b_h, start=False, stop=False)
                    return pe.matmul(o, a_h, b_l, start=False, stop=stop)

                def transpose_patches(part, p, at, ns):
                    for n in ns:
                        c, w0, nw = TSTEPS[n]
                        if w0 == 0:
                            pe.wait_ge(patched, p * 3 + c + 1)
                        b, d = begin(part, "T", n, at)
                        for w in range(nw):
                            mm = pe.transpose(d[:, w * 2 * ROWS:(w + 1) * 2 * ROWS], patches[:, c, w0 + w, :], ident[0:2 * ROWS, 0:2 * ROWS])
                        mm.then_inc(dense_full[b], 1)

                def embed(part, p, at, t):
                    if t == 0:
                        pe.wait_ge(halo_copied, p)
                    b, _ = fill(part, "E", t // 2, at)
                    if t % 2 == 0:
                        begin(part, "E", t // 2, at)
                    for k in range(KC):
                        mm = product(dense[b][:, (t % 2) * 256:(t % 2) * 256 + 256],
                                     xT_h[:, k, t * 128:t * 128 + 128], xT_l[:, k, t * 128:t * 128 + 128],
                                     wp_h[:, k * C:(k + 1) * C], wp_l[:, k * C:(k + 1) * C],
                                     k == 0, k == KC - 1)
                    if t in (tiles[-1] for tiles in PAIRS):
                        mm.then_inc(dense_full[b], 1)

                def turn(part, stage, at, n, src, order):
                    b, d = begin(part, stage, n, at)
                    for t in PAIRS[n]:
                        for m in range(MC):
                            to = (t % 2) * 256 + m * 128
                            mm = pe.transpose(d[:, to:to + 128], src[:, t, m * 128:m * 128 + 128], order[:, :])
                    mm.then_inc(dense_full[b], 1)

                def hn_to_channels(part, g, n):
                    pe.wait_ge(hn_ready, g * 4 + n + 1)
                    turn(part, "N", g, n, hn, ident)

                def hn2_to_channels(part, g, at, n):
                    pe.wait_ge(hn2_ready, g * 4 + n + 1)
                    turn(part, "L", at, n, hn2, own_first)

                def queries_keys(part, g, n):
                    if n == 0:
                        wait_read(pe, part, "N", 3, g)
                    m, rest = divmod(n, 4)
                    of, u = divmod(rest, 2)
                    b, d = begin(part, "Q", n, g)
                    for k in range(MC):
                        at = k * 3 * C + of * C + m * 128
                        hh, hl = (own(a[:, k], u) for a in (hnT_h, hnT_l))
                        mm = product(d[:, 0:UT], wqkv_h[:, at:at + 128], wqkv_l[:, at:at + 128], hh, hl,
                                     k == 0, k == MC - 1)
                    mm.then_inc(dense_full[b], 1)

                def values(part, g, n):
                    b, d = begin(part, "V", n, g)
                    for t in PAIRS[n]:
                        for k in range(MC):
                            at = k * 3 * C + 2 * C
                            mm = product(d[:, (t % 2) * 256:(t % 2) * 256 + 256],
                                         hnT_h[:, k, t * 128:t * 128 + 128], hnT_l[:, k, t * 128:t * 128 + 128],
                                         wqkv_h[:, at:at + C], wqkv_l[:, at:at + C], k == 0, k == MC - 1)
                    mm.then_inc(dense_full[b], 1)

                def scores(part, g, hc, hq):
                    if hq == 0:
                        pe.wait_ge(keys_whole, g * MC + hc + 1)
                    if hc > 0:
                        pe.wait_ge(scores_read, g * 8 + hq + 1)
                    settle(pe)
                    for t in range(TILES):
                        for b in range(4):
                            cols = slice(t * 128 + b * POS, t * 128 + b * POS + POS)
                            at = (hc * TILES + t) * POS
                            mm = pe.matmul(att[hq][b * 32:b * 32 + 32, at:at + POS],
                                           qT[hq * 32:hq * 32 + 32, hc, cols],
                                           kT[hq * 32:hq * 32 + 32, hc, cols], start=True, stop=True,
                                           tile_position=(hq * 32, b * 32))
                    mm.then_inc(scores_ready, 1)

                def attend(part, g, hc, b):
                    if b == 0:
                        wait_read(pe, part, "V", 3, g)
                        pe.wait_ge(pT_ready, g * 2 + hc + 1)
                    if hc == 0 and b == 0:
                        pe.wait_ge(scores_read, g * 8 + 8)
                    if hc == 0 and b == 3 and part != "zero":
                        pe.wait_ge(gshifted, g)
                    settle(pe)
                    for t in range(TILES):
                        for hq in range(HQ):
                            h = hc * HQ + hq
                            at = (hc * TILES + t) * POS
                            mm = pe.matmul(att[b][hq * 32:hq * 32 + 32, at:at + POS],
                                           v[b * 32:b * 32 + 32, t, h * DH:h * DH + DH],
                                           pT[b * 32:b * 32 + 32, h * TILES + t, :], start=True, stop=True,
                                           tile_position=(b * 32, hq * 32))
                    if hc == MC - 1:
                        mm.then_inc(attended, 1)

                def project(part, g, at, n):
                    if n == 0:
                        pe.wait_ge(oT_lo, g * 4 + 4)
                    b, d = begin(part, "O", n, at)
                    for t in PAIRS[n]:
                        for m in range(MC):
                            mm = product(d[:, (t % 2) * 256:(t % 2) * 256 + 256], oT_h[:, t, m, :], oT_l[:, t, m, :],
                                         wo_h[:, m * C:(m + 1) * C], wo_l[:, m * C:(m + 1) * C], m == 0, m == MC - 1)
                    mm.then_inc(dense_full[b], 1)

                def gates(part, g, at, n):
                    if n == 0:
                        if part != "end":
                            pe.wait_ge(scores_read, g * 8 + 16)
                        pe.matmul(att[3][0:OWN, 0:TILES * E], ones[:, 0:OWN], view(bgs[:, 0, 0:1], [1, TILES * E]), start=True, stop=False)
                    wait_read(pe, part, "L", n, at)
                    for t in PAIRS[n]:
                        for m in range(MC):
                            mm = pe.matmul(att[3][0:OWN, t * E:(t + 1) * E], hn2T[:, m, t * OWN:(t + 1) * OWN], wgs[:, m, :],
                                           start=False, stop=(t == TILES - 1 and m == MC - 1))
                    if n == 3:
                        mm.then_inc(gates_done, 1)

                def iteration(part, g):
                    for name, n in until(part, "Q", 4):
                        if name == "T":
                            transpose_patches(part, g + 1, g, [n])
                        elif name == "O":
                            project(part, g - 1, g, n)
                        elif name == "N":
                            hn_to_channels(part, g, n)
                        else:
                            queries_keys(part, g, n)
                    for n in range(4):
                        queries_keys(part, g, 4 + n)
                        scores(part, g, 0, n)
                    for n in range(4):
                        values(part, g, n)
                        scores(part, g, 1, n)
                    if part != "zero":
                        for n in range(4):
                            hn2_to_channels(part, g - 1, g, n)
                    for n in range(8):
                        if part != "last" and n < TILES:
                            embed(part, g + 1, g, n)
                        if part != "zero":
                            for pair in ((0,), (1,), (2, 3))[n] if n < 3 else ():
                                gates(part, g - 1, g, pair)
                        attend(part, g, n // 4, n % 4)

                pe.wait_ge(setup, 1)
                pe.wait_ge(ident_in, 16)

                def embed_first(c):
                    pe.wait_ge(first_halo, c + 1)
                    for n, tiles in enumerate(PAIRS):
                        for t in tiles:
                            for k in (2 * c, 2 * c + 1):
                                mm = product(att[n][:, (t % 2) * 256:(t % 2) * 256 + 256],
                                             xT_h[:, k, t * 128:t * 128 + 128], xT_l[:, k, t * 128:t * 128 + 128],
                                             wp_h[:, k * C:(k + 1) * C], wp_l[:, k * C:(k + 1) * C],
                                             k == 0 and t == tiles[0], k == KC - 1 and t == tiles[-1])
                        if c == 2:
                            mm.then_inc(first_embedded, 1)

                transpose_patches("first", 0, 0, range(8))
                pe.wait_ge(weights_low, 1)
                embed_first(0)
                transpose_patches("first", 0, 0, range(8, 12))
                embed_first(1)
                embed_first(2)
                pe.wait_ge(weights_low, 3)
                pe.wait_ge(consts_in, 16 * 11)
                iteration("zero", 0)
                with pe.Fori(1, G - 1) as g:
                    iteration("loop", g)
                iteration("last", G - 1)
                for n in range(4):
                    project("end", G - 1, G - 1, n)
                for n in range(4):
                    hn2_to_channels("end", G - 1, G - 1, n)
                for n in range(4):
                    gates("end", G - 1, G - 1, n)

            @block.scalar
            def _(act):
                def full(part, stage, n, g):
                    b, turns = fill(part, stage, n, g)
                    act.wait_ge(dense_full[b], turns + 1)
                    return b, dense[b]

                def patches_high(part, p, at, ns):
                    for n in ns:
                        c, w0, nw = TSTEPS[n]
                        b, d = full(part, "T", n, at)
                        src, dst = patch_views(d, xT_h, c, w0, nw)
                        act.activation(dst, src, ACT.Copy).then_inc(xT_hi, 1)

                def normalise(n, g, src, dst, ready):
                    act.wait_ge(shift_ready[n], g + 1)
                    for t in range(TILES):
                        ins = act.activation(dst[:, t, :], src[:, t, :], ACT.Identity, scale=rstd[n][:, t:t + 1],
                                             bias=shift[n][:, t:t + 1])
                        if t % 2 or t == TILES - 1:
                            ins.then_inc(ready, 1)

                def hn_high(part, g, n):
                    b, d = full(part, "N", n, g)
                    src, dst = channel_views(d, hnT_h, PAIRS[n])
                    act.activation(dst, src, ACT.Copy).then_inc(hnT_hi, 1)

                def qk_out(part, g, ns):
                    for n in ns:
                        m, rest = divmod(n, 4)
                        of, u = divmod(rest, 2)
                        b, d = full(part, "Q", n, g)
                        act.activation(own((qT, kT)[of][:, m], u), d[:, 0:UT].rearrange("p (b i) -> p b i", i=Q),
                                       ACT.Copy).then_inc(dense_free[b], 1)
                        if of and u:
                            wait_read(act, part, "Q", n - 1, g)
                            wait_read(act, part, "Q", n, g)
                            for to, of_pos in ((POS, Q), (Q + HALO, POS + HALO)):
                                ins = act.activation(view(kT[:, m, to:to + 1], [POS, BLOCKS - 1], [1, HALO]),
                                                     view(kT[:, m, of_pos:of_pos + 1], [POS, BLOCKS - 1], [1, HALO]), ACT.Copy)
                            ins.then_inc(keys_whole, 1)

                def v_out(part, g, ns):
                    for n in ns:
                        tiles = PAIRS[n]
                        b, d = full(part, "V", n, g)
                        act.activation(view(v[:, tiles[0], 0:1], [1, 256 * len(tiles)]), d[:, 0:256 * len(tiles)],
                                       ACT.Copy).then_inc(dense_free[b], 1)

                def softmax_exp(g, hc):
                    act.wait_ge(shifted, g * 2 + hc + 1)
                    w = view(win[:, hc, 0, 0, 0:1], [1, 2 * HIDX * 6])
                    act.activation(w, w, ACT.Exp, scale=SCALE).then_inc(exped, 1)

                def attended_high(g):
                    for n in range(4):
                        act.wait_ge(attended, g * 4 + n + 1)
                        src, dst = attended_views(att[n], oT_h, n)
                        act.activation(dst, src, ACT.Copy).then_inc(oT_hi, 1)

                def hn2_out(part, g, at):
                    act.wait_ge(hn2T_stored, g * 16 + 1)
                    for n, tiles in enumerate(PAIRS):
                        b, d = full(part, "L", n, at)
                        src, dst = channel_views(d, hn2T, tiles, OWN)
                        act.activation(dst, src, ACT.Copy).then_inc(dense_free[b], 1)

                def gate_exp(g):
                    act.wait_ge(gshifted, g + 1)
                    w = view(gate[:, 0, 0:1], [1, TILES * E])
                    act.activation(w, w, ACT.Exp).then_inc(gexped, 1)

                def iteration(part, g):
                    if part != "last":
                        patches_high(part, g + 1, g, range(3))
                    normalise(0, g, hpos, hn, hn_ready)
                    for name, n in until(part, "V", 0):
                        if name == "T" and n >= 3:
                            patches_high(part, g + 1, g, [n])
                        elif name == "N":
                            hn_high(part, g, n)
                        elif name == "Q":
                            qk_out(part, g, [n])
                    if part != "zero":
                        normalise(1, g - 1, h2, hn2, hn2_ready)
                    v_out(part, g, (0, 1))
                    softmax_exp(g, 0)
                    v_out(part, g, (2, 3))
                    if part != "zero":
                        hn2_out(part, g - 1, g)
                    softmax_exp(g, 1)
                    if part != "zero":
                        gate_exp(g - 1)
                    attended_high(g)

                for n, src in enumerate((w_patch, w_qkv, w_out)):
                    act.dma_start(WEIGHTS[n][2], src).then_inc(weight_in[n], 16)
                for dst, src in ((own_first[:, :], c_own_first), (band[:, :], c_band), (window[:, :], c_window), (there[:, :], c_there),
                                 (windows[:, :], c_windows), (lower[:, :], c_lower), (same[:, :], c_same),
                                 (view(wgs[:, 0, 0:1], [1, MC * E]), w_gate),
                                 (b_embed[:, :], copies(b_patch, 128)), (view(six[:, 0, 0:1], [1, C]), copies(b_out, 128)),
                                 (view(bgs[:, 0, 0:1], [E, TILES], [1, E]), copies(b_gate, 1, TILES))):
                    act.dma_start(dst, src).then_inc(consts_in, 16)

                def weight_high(n):
                    hi, _, src = WEIGHTS[n]
                    act.wait_ge(weight_in[n], 16)
                    act.activation(hi[:, :], src, ACT.Copy).then_inc(weights_high, 1)

                weight_high(0)
                patches_high("first", 0, 0, range(12))
                weight_high(1)
                weight_high(2)
                iteration("zero", 0)
                with act.Fori(1, G - 1) as g:
                    iteration("loop", g)
                iteration("last", G - 1)
                normalise(1, G - 1, h2, hn2, hn2_ready)
                hn2_out("end", G - 1, G - 1)
                gate_exp(G - 1)

            @block.vector
            def _(dve):
                ln = [Steps(dve, ln_step[n], 2) for n in range(2)]
                soft = Steps(dve, soft_step, SOFT_STEPS)
                gs = Steps(dve, gate_step, 9)

                def full(part, stage, n, g):
                    b, turns = fill(part, stage, n, g)
                    dve.wait_ge(dense_full[b], turns + 1)
                    return b, dense[b]

                def patches_low(part, p, at, ns):
                    for n in ns:
                        c, w0, nw = TSTEPS[n]
                        dve.wait_ge(xT_hi, p * 12 + n + 1)
                        b, d = full(part, "T", n, at)
                        src, hi = patch_views(d, xT_h, c, w0, nw)
                        lo = patch_views(d, xT_l, c, w0, nw)[1]
                        dve.tensor_tensor(lo, src, hi.bitcast(F32), ALU.subtract).then_inc(dense_free[b], 1)

                def bias_add(n, d):
                    tiles = PAIRS[n]
                    return dve.tensor_tensor(view(hpos[:, tiles[0], 0:1], [C, len(tiles)], [1, C]),
                                             view(d[:, 0:1], [C, len(tiles)], [1, C]),
                                             view(b_embed[:, 0:1], [0, len(tiles)], [1, C]), ALU.add)

                def embed_out(part, p, at, ns):
                    if ns[0] == 0:
                        dve.wait_ge(h2_begun, p)
                    for n in ns:
                        b, d = full(part, "E", n, at)
                        bias_add(n, d).then_inc(dense_free[b], 1)

                def statistics(n, g, src, tiles=range(TILES), between=None):
                    s = ln[n]
                    s.group(g)
                    for t in tiles:
                        ins = dve.bn_stats(stat[n][:, t, :], src[:, t, :])
                    if TILES - 1 not in tiles:
                        return
                    s.did(ins)
                    if between is not None:
                        between()
                    s.wait()
                    settle(dve)
                    for t in range(TILES):
                        ins = dve.bn_aggr(mv[n][:, t, :], stat[n][:, t, :])
                    s.did(ins)
                    s.wait()
                    dve.tensor_scalar(negmean[n][:, :], mv[n][:, :, 0], -1.0, None, ALU.mult)
                    dve.tensor_scalar(vare[n][:, :], mv[n][:, :, 1], LN_EPS, None, ALU.add).then_inc(var_ready[n], 1)
                    s.end()

                def hn_low(part, g, n):
                    dve.wait_ge(hnT_hi, g * 4 + n + 1)
                    b, d = full(part, "N", n, g)
                    src, hi = channel_views(d, hnT_h, PAIRS[n])
                    lo = channel_views(d, hnT_l, PAIRS[n])[1]
                    dve.tensor_tensor(lo, src, hi.bitcast(F32), ALU.subtract).then_inc(dense_free[b], 1)

                def softmax_shift(g, hc):
                    s = soft
                    s.group(g * 2 + hc)
                    n = TILES
                    for hq in range(HQ):
                        dve.wait_ge(scores_ready, g * 8 + hc * 4 + hq + 1)
                        at = hc * HIDX + hq * n
                        ins = dve.tensor_tensor(banded[:, at:at + n, 0:POS],
                                                att[hq][:, hc * n * POS:(hc + 1) * n * POS].rearrange("p (k j) -> p k j", j=POS),
                                                view(band[:, 0:1], [0, n], [1, POS]), ALU.mult).then_inc(scores_read, 1)
                    dve.wait_ge(scores_read, g * 8 + hc * 4 + 4)
                    at = hc * HIDX
                    s.did(dve.tensor_reduce(six[:, at:at + HIDX, :], view(banded[:, at, 0:1], [BAND, HIDX], [1, 6], [6, BAND // 6]),
                                            AX.X, ALU.add))
                    s.wait()
                    for w in range(2):
                        ins = dve.tensor_tensor(win[:, hc, w], six[:, at:at + HIDX, :],
                                                view(window[:, 6 * w:6 * w + 1], [0, HIDX], [1, 6]), ALU.add)
                    s.did(ins)
                    s.wait()
                    flat = view(win[:, hc, 0, 0, 0:1], [6, 2 * HIDX], [1, 6])
                    s.did(dve.tensor_reduce(wstat[:, hc, :], flat, AX.X, ALU.max))
                    s.wait()
                    dve.tensor_tensor(flat, flat, view(wstat[:, hc, 0:1], [1, 2 * HIDX], [0, 6]), ALU.subtract).then_inc(shifted, 1)

                def softmax_weigh(g, hc):
                    s = soft
                    at = hc * HIDX
                    flat = view(win[:, hc, 0, 0, 0:1], [6, 2 * HIDX], [1, 6])
                    per = view(wstat[:, hc, 0:1], [1, 2 * HIDX], [0, 6])
                    dve.wait_ge(exped, g * 2 + hc + 1)
                    s.did(dve.tensor_reduce(wstat[:, hc, :], flat, AX.X, ALU.add))
                    s.wait()
                    s.did(dve.reciprocal(wstat[:, hc, :], wstat[:, hc, :]))
                    s.wait()
                    s.did(dve.tensor_tensor(wstat[:, hc, :], wstat[:, hc, :], there[:, :], ALU.mult))
                    s.wait()
                    s.did(dve.tensor_tensor(flat, flat, per, ALU.mult))
                    s.wait()
                    s.did(dve.tensor_tensor(prob[:, at:at + HIDX, :], win[:, hc, 0], win[:, hc, 1], ALU.add))
                    s.wait()
                    dve.tensor_tensor(view(banded[:, at, 0:1], [BAND, HIDX], [6, BAND // 6], [1, 6]),
                                      view(prob[:, at, 0:1], [6, HIDX], [0, BAND // 6], [1, 6]),
                                      view(band[:, 0:1], [0, HIDX], [6, BAND // 6], [1, 6]), ALU.mult).then_inc(spread_done, 1)
                    dve.wait_ge(spread_done, g * 2 + hc + 1)
                    dve.transpose(pT[:, at:at + HIDX, :], banded[:, at:at + HIDX, 0:POS]).then_inc(pT_ready, 1)
                    s.end()

                def attended_low(g, ns):
                    for n in ns:
                        dve.wait_ge(oT_hi, g * 4 + n + 1)
                        src, hi = attended_views(att[n], oT_h, n)
                        lo = attended_views(att[n], oT_l, n)[1]
                        dve.tensor_tensor(lo, src, hi.bitcast(F32), ALU.subtract).then_inc(oT_lo, 1)

                def residual(part, g, at, n):
                    if n == 0:
                        dve.wait_ge(h2_begun, g + 1)
                    b, d = full(part, "O", n, at)
                    w = [1, 256 * len(PAIRS[n])]
                    dve.tensor_tensor(view(h2[:, PAIRS[n][0], 0:1], w), d[:, 0:256 * len(PAIRS[n])],
                                      view(h2[:, PAIRS[n][0], 0:1], w), ALU.add).then_inc(dense_free[b], 1)

                def gates_shift(g):
                    s = gs
                    s.group(g)
                    dve.wait_ge(gates_done, g + 1)
                    logits = att[3][0:OWN, 0:TILES * E].rearrange("p (t e) -> p t e", e=E)
                    s.did(dve.tensor_reduce(gstat[:, 0:TILES], logits, AX.X, ALU.max))
                    s.wait()
                    dve.tensor_tensor(gate[:, :, :], logits, view(gstat[:, 0:1], [1, TILES], [0, E]), ALU.subtract).then_inc(gshifted, 1)

                def route_gates(g):
                    s = gs
                    dve.wait_ge(gexped, g + 1)
                    dve.wait_ge(scoresT_stored, g * 128 + 1)
                    s.did(dve.tensor_reduce(gstat[:, 0:TILES], gate[:, :, :], AX.X, ALU.add))
                    s.wait()
                    s.did(dve.reciprocal(gstat[:, TILES:2 * TILES], gstat[:, 0:TILES]))
                    s.wait()
                    s.did(dve.tensor_tensor(gate[:, :, :], gate[:, :, :], view(gstat[:, TILES:TILES + 1], [1, TILES], [0, E]), ALU.mult))
                    s.wait()
                    mine = view(gate[:, 0, 0:1], [E, TILES], [1, E], [0, E])
                    other = view(gate[:, 0, 0:1], [E, TILES], [0, E], [1, E])
                    dve.tensor_tensor(above[:, :, :, :], other, mine, ALU.is_gt)
                    s.did(dve.tensor_tensor(level[:, :, :, :], other, mine, ALU.is_equal))
                    s.wait()
                    flat = lambda a: view(a[:, 0, 0, 0:1], [E * E, TILES], [1, E * E])
                    s.did(dve.tensor_tensor(flat(level), flat(level), view(lower[0:OWN, 0:1], [0, TILES], [1, E * E]), ALU.mult))
                    s.wait()
                    s.did(dve.tensor_tensor(flat(above), flat(above), flat(level), ALU.add))
                    s.wait()
                    s.did(dve.tensor_reduce(rank[:, :, :], above[:, :, :, :], AX.X, ALU.add))
                    s.wait()
                    both = view(masked[0:OWN, 0:1], [1, TILES * E])
                    s.did(dve.scalar_tensor_tensor(both, view(rank[:, 0, 0:1], [1, TILES * E]), TOPK - 0.5,
                                                   view(gate[:, 0, 0:1], [1, TILES * E]), ALU.is_lt, ALU.mult))
                    s.wait()
                    dve.transpose(scoresT[:, :], masked[:, :]).then_inc(scoresT_ready, 1)
                    s.end()

                def weight_low(n):
                    hi, lo, src = WEIGHTS[n]
                    dve.wait_ge(weights_high, n + 1)
                    dve.tensor_tensor(lo[:, :], src, hi[:, :].bitcast(F32), ALU.subtract).then_inc(weights_low, 1)

                weight_low(0)
                patches_low("first", 0, 0, range(12))
                weight_low(1)
                weight_low(2)
                dve.wait_ge(setup, 1)
                dve.wait_ge(consts_in, 16 * 11)
                for t in range(TILES):
                    last = dve.tensor_scalar(b_attn[:, t, :], view(six[:, 0, 0:1], [1, C]), windows[:, t:t + 1], None, ALU.mult)
                last.then_inc(bias_spread, 1)
                for n, tiles in enumerate(PAIRS):
                    dve.wait_ge(first_embedded, n + 1)
                    bias_add(n, att[n]).then_inc(first_read, 1)
                dve.wait_ge(first_read, 4)
                statistics(0, 0, hpos)

                def iteration(part, g):
                    for name, n in until(part, "Q", 4):
                        if name == "T":
                            patches_low(part, g + 1, g, [n])
                        elif name == "O":
                            residual(part, g - 1, g, n)
                        elif name == "N":
                            hn_low(part, g, n)
                    if part != "zero":
                        wait_read(dve, part, "O", 3, g)
                        statistics(1, g - 1, h2)
                    softmax_shift(g, 0)
                    softmax_weigh(g, 0)
                    softmax_shift(g, 1)
                    softmax_weigh(g, 1)
                    if part != "zero":
                        gates_shift(g - 1)
                        route_gates(g - 1)
                    if part != "last":
                        embed_out(part, g + 1, g, (0, 1))
                        wait_read(dve, part, "E", 1, g)
                        statistics(0, g + 1, hpos, range(0, 4))
                    attended_low(g, (0, 1))
                    if part != "last":
                        embed_out(part, g + 1, g, (2, 3))
                        wait_read(dve, part, "E", 3, g)
                        statistics(0, g + 1, hpos, range(4, TILES), lambda: attended_low(g, (2,)))
                    attended_low(g, (2, 3) if part == "last" else (3,))

                iteration("zero", 0)
                with dve.Fori(1, G - 1) as g:
                    iteration("loop", g)
                iteration("last", G - 1)
                for n in range(4):
                    residual("end", G - 1, G - 1, n)
                wait_read(dve, "end", "O", 3, G - 1)
                statistics(1, G - 1, h2)
                gates_shift(G - 1)
                route_gates(G - 1)

        scores_in = [sem(f"scores_in{c}") for c in range(CH)]
        summed, route_step, loop_step = sem("summed"), sem("route_step"), sem("loop_step")
        picked_ready, picked_stored = sem("picked_ready"), sem("picked_stored")
        w1_in, ffn_in, zeroed = sem("w1_in"), sem("ffn_in"), sem("zeroed")
        w_high, w_low = sem("w_high"), sem("w_low")
        t_in_loaded, t_high, t_low = sem("t_in_loaded"), sem("t_high"), sem("t_low")
        mask_loaded, mask_used = sem("mask_loaded"), sem("mask_used")
        unit_mask_loaded, b2_split = sem("unit_mask_loaded"), sem("b2_split")
        h_loaded, y_full, y_added, y_stored = sem("h_loaded"), sem("y_full"), sem("y_added"), sem("y_stored")
        hid_full, activated = sem("hid_full"), sem("activated")
        mask_put = sem("mask_put")
        hid_high, hid_low = sem("hid_high"), sem("hid_low")
        STEPS3 = [(u, c) for u in range(2) for c in range(HID)]
        N3 = len(STEPS3)
        out_t = out.rearrange("(g t p) n -> g p t n", t=TILES, p=OWN)

        with nc.Block() as block:
            def rows(dram, c):
                return bass.AP(dram.tensor, dram.offset + c * CIMG * SEQ, [[SEQ, CIMG], [NTOK, E], [1, SEQ]])

            @block.sync
            def _(sp):
                def load_t(i):
                    sp.dma_start(view(t_in[:, 0, 0:1], [1, MC * TOK]), h2n_d[i]).then_inc(t_in_loaded, 16)

                def load_mask(i):
                    for n in range(3):
                        sp.dma_start(mask16[n * GAP:n * GAP + E, :], mask_d[:, bass.ds(i * TOK, TOK)]).then_inc(mask_loaded, 16)

                def load_unit_mask(i):
                    for c in range(HID):
                        row = mask_d[c * 128 // SUB:(c + 1) * 128 // SUB, bass.ds(i * TOK, TOK)]
                        src = bass.AP(row.tensor, row.offset, [list(row.ap[0]), [0, SUB], list(row.ap[1])])
                        sp.dma_start(unit_mask[:, c, :], src).then_inc(unit_mask_loaded, 16)

                def load_h(i):
                    sp.dma_start(h_in[:, :, :], out_t[i]).then_inc(h_loaded, 16)

                def store(i):
                    sp.wait_ge(y_added, i * 4 + 4)
                    sp.dma_start(out_t[i], y_out[:, :, :]).then_inc(y_stored, 16)

                sp.sem_inc(y_stored, 1)
                for c in range(CH):
                    sp.dma_start(route[:, c, 0:SEQ], rows(score_d, c)).then_inc(scores_in[c], 16)
                sp.dma_start(w1s[:, :], w1).then_inc(w1_in, 16)
                load_t(0)
                for dst, src in ((b1s, b1), (w2s, w2)):
                    sp.dma_start(dst[:, :], src).then_inc(ffn_in, 16)
                sp.wait_ge(zeroed, 1)
                for n in range(3):
                    sp.dma_start(b2_left[n * GAP:n * GAP + E, :], b2).then_inc(ffn_in, 16)
                load_h(0)
                def masks(c):
                    sp.wait_ge(picked_ready, 1 + c * GPC)
                    sp.dma_start(rows(mask_d, c), picked[:, c, :]).then_inc(picked_stored, 16)
                    sp.wait_ge(picked_stored, c * 16 + 16)

                def step(i, last=False):
                    sp.wait_ge(t_low, i + 1)
                    load_t(i + 1)
                    if last:
                        masks((i + 1) // GPC)
                    sp.wait_ge(mask_put, i * N3 + N3)
                    load_unit_mask(i + 1)
                    sp.wait_ge(mask_used, i + 1)
                    load_mask(i + 1)
                    store(i)
                    load_h(i + 1)

                masks(0)
                load_unit_mask(0)
                load_mask(0)
                for c in range(CH):
                    with sp.Fori(c * GPC, c * GPC + GPC - 1) as i:
                        step(i)
                    if c < CH - 1:
                        step(c * GPC + GPC - 1, last=True)
                store(G - 1)
                sp.wait_ge(y_stored, G * 16 + 1)

            @block.tensor
            def _(pe):
                def product(o, a_h, a_l, b_h, b_l, start, stop):
                    pe.matmul(o, a_h, b_h, start=start, stop=False)
                    pe.matmul(o, a_l, b_h, start=False, stop=False)
                    return pe.matmul(o, a_h, b_l, start=False, stop=stop)

                def hidden(i, n):
                    u, c = STEPS3[n]
                    if n >= 4:
                        pe.wait_ge(activated, i * N3 + n - 3)
                    for k in range(MC):
                        at = k * E * SUB + c * 128
                        th, tl = (t[:, k, u * UT:(u + 1) * UT] for t in (t_h, t_l))
                        mm = product(bank[n % 4][:, 0:UT], w1_h[:, at:at + 128], w1_l[:, at:at + 128], th, tl,
                                     k == 0, k == MC - 1)
                    mm.then_inc(hid_full, 1)

                def outputs(i):
                    def place(t):
                        return bank[4 + t // 2][0:OWN, (t % 2) * 256:(t % 2) * 256 + 256], slice(t * OWN, (t + 1) * OWN)

                    pe.wait_ge(hid_low, i * N3 + HID)
                    for t in range(TILES):
                        o, cols = place(t)
                        mm = pe.matmul(o, mask16[:, cols], b2_parts[:, :], start=(t % 2 == 0), stop=False)
                    mm.then_inc(mask_used, 1)
                    for n, tiles in enumerate(PAIRS):
                        if n > 0:
                            pe.wait_ge(hid_low, i * N3 + N3)
                        for t in tiles:
                            o, cols = place(t)
                            for c in range(HID):
                                mm = product(o, hid_h[:, c, cols], hid_l[:, c, cols], w2_h[:, c * C:(c + 1) * C],
                                             w2_l[:, c * C:(c + 1) * C], False, c == HID - 1 and t == tiles[-1])
                        mm.then_inc(y_full, 1)

                for c in range(CH):
                    pe.wait_ge(scores_in[c], 16)
                    mm = pe.matmul(bank[7][:, 0:SEQ], same[:, :], route[:, c, 0:SEQ], start=(c == 0), stop=(c == CH - 1))
                mm.then_inc(summed, 1)
                pe.wait_ge(w_low, 1)
                pe.wait_ge(t_low, 1)
                for n in range(N3):
                    hidden(0, n)
                pe.wait_ge(mask_loaded, 48)
                pe.wait_ge(w_low, 2)
                pe.wait_ge(b2_split, 5)
                outputs(0)
                with pe.Fori(1, G) as i:
                    pe.wait_ge(t_low, i + 1)
                    for n in range(N3):
                        hidden(i, n)
                    pe.wait_ge(mask_loaded, i * 48 + 48)
                    outputs(i)

            @block.scalar
            def _(act):
                def split_high(i):
                    act.wait_ge(t_in_loaded, i * 16 + 16)
                    act.activation(t_h[:, :, :], t_in[:, :, :], ACT.Copy).then_inc(t_high, 1)

                def high(i, n):
                    u, c = STEPS3[n]
                    act.wait_ge(mask_put, i * N3 + n + 1)
                    act.activation(hid_h[:, c, u * UT:(u + 1) * UT], hid[:, c, u * UT:(u + 1) * UT],
                                   ACT.Copy).then_inc(hid_high, 1)

                def gelu(i, n):
                    u, c = STEPS3[n]
                    act.wait_ge(hid_full, i * N3 + n + 1)
                    act.activation(hid[:, c, u * UT:(u + 1) * UT], bank[n % 4][:, 0:UT], ACT.Gelu,
                                   bias=b1s[:, c:c + 1]).then_inc(activated, 1)

                def group(i):
                    for n in range(N3):
                        gelu(i, n)
                        if n > 0:
                            high(i, n - 1)
                    high(i, N3 - 1)

                act.wait_ge(w1_in, 16)
                act.activation(w1_h[:, :], w1s[:, :], ACT.Copy).then_inc(w_high, 1)
                split_high(0)
                act.wait_ge(ffn_in, 16 * 5)
                act.activation(w2_h[:, :], w2s[:, :], ACT.Copy).then_inc(w_high, 1)
                for n in range(N3):
                    gelu(0, n)
                for n in range(N3):
                    high(0, n)
                split_high(1)
                with act.Fori(1, G - 1) as i:
                    group(i)
                    split_high(i + 1)
                group(G - 1)

            @block.vector
            def _(dve):
                def split_low(i):
                    dve.wait_ge(t_high, i + 1)
                    dve.tensor_tensor(t_l[:, :, :], t_in[:, :, :], t_h[:, :, :].bitcast(F32), ALU.subtract).then_inc(t_low, 1)

                def low(i, n):
                    u, c = STEPS3[n]
                    cols = slice(u * UT, (u + 1) * UT)
                    dve.wait_ge(hid_high, i * N3 + n + 1)
                    dve.tensor_tensor(hid_l[:, c, cols], hid[:, c, cols], hid_h[:, c, cols].bitcast(F32),
                                      ALU.subtract).then_inc(hid_low, 1)

                def group(i):
                    for n, (u, c) in enumerate(STEPS3):
                        cols = slice(u * UT, (u + 1) * UT)
                        dve.wait_ge(activated, i * N3 + n + 1)
                        if n == 0:
                            dve.wait_ge(unit_mask_loaded, i * 64 + 64)
                        dve.tensor_tensor(hid[:, c, cols], unit_mask[:, c, cols], hid[:, c, cols],
                                          ALU.mult).then_inc(mask_put, 1)
                        if n > 0:
                            low(i, n - 1)
                    low(i, N3 - 1)

                def add(i):
                    dve.wait_ge(h_loaded, i * 16 + 16)
                    dve.wait_ge(y_stored, i * 16 + 1)
                    for n, tiles in enumerate(PAIRS):
                        dve.wait_ge(y_full, i * 4 + n + 1)
                        w = [1, 256 * len(tiles)]
                        dve.tensor_tensor(view(y_out[:, tiles[0], 0:1], w), bank[4 + n][0:OWN, 0:256 * len(tiles)],
                                          view(h_in[:, tiles[0], 0:1], w), ALU.add).then_inc(y_added, 1)

                def split_bias():
                    dve.wait_ge(ffn_in, 16 * 5)
                    dve.tensor_copy(b2_parts[:, :], b2_left[:, :]).then_inc(b2_split, 1)
                    dve.wait_ge(b2_split, 1)
                    for at in (GAP, 2 * GAP):
                        last = dve.tensor_tensor(b2_left[at:at + GAP, :], b2_left[at:at + GAP, :], b2_parts[at:at + GAP, :], ALU.subtract)
                    last.then_inc(b2_split, 1)
                    dve.wait_ge(b2_split, 2)
                    for at in (GAP, 2 * GAP):
                        last = dve.tensor_copy(b2_parts[at:at + GAP, :], b2_left[at:at + GAP, :])
                    last.then_inc(b2_split, 1)
                    dve.wait_ge(b2_split, 3)
                    third = slice(2 * GAP, 3 * GAP)
                    dve.tensor_tensor(b2_left[third, :], b2_left[third, :], b2_parts[third, :], ALU.subtract).then_inc(b2_split, 1)
                    dve.wait_ge(b2_split, 4)
                    dve.tensor_copy(b2_parts[third, :], b2_left[third, :]).then_inc(b2_split, 1)

                def pick(s, c, looped=True):
                    s.did(dve.max(best[:, c, :], route[:, c, :]))
                    s.wait()
                    if looped:
                        settle(dve)
                    s.did(dve.match_replace(route[:, c, :], best[:, c, :], route[:, c, :], -1.0))
                    s.wait()
                    if looped:
                        settle(dve)

                def show_picked(c):
                    dve.tensor_scalar(picked[:, c, :], route[:, c, 0:SEQ], 0.0, None, ALU.is_lt).then_inc(picked_ready, 1)

                def weigh(s, c):
                    s.did(dve.scalar_tensor_tensor(route[:, c, 0:SEQ], route[:, c, 0:SEQ], float(B), rden[:, :], ALU.mult, ALU.mult))
                    s.wait()

                def rank_first():
                    s = Steps(dve, route_step, 3 + CH + 2 * ROUNDS)
                    s.group(0)
                    first = ROUNDS * 8 - PICK
                    dve.memset(route[:, 0, SEQ:SEQ + first], BIG)
                    last = dve.memset(route[:, 0, SEQ + first:SEQ + PAD], -1.0)
                    if CH > 1:
                        last = dve.memset(route[:, 1:, SEQ:SEQ + PAD], BIG)
                    s.did(last)
                    dve.wait_ge(summed, 1)
                    s.did(dve.tensor_scalar(rden[:, :], bank[7][:, 0:SEQ], GATE_EPS, None, ALU.add))
                    s.wait()
                    s.did(dve.reciprocal(rden[:, :], rden[:, :]))
                    s.wait()
                    weigh(s, 0)
                    for _ in range(ROUNDS):
                        pick(s, 0, looped=False)
                    show_picked(0)
                    for c in range(1, CH):
                        weigh(s, c)
                    s.end()

                loop = Steps(dve, loop_step, 2 * LOOP_ROUNDS // GPC)

                def step(i, c):
                    group(i)
                    if c < CH:
                        loop.group(i)
                        for _ in range(LOOP_ROUNDS // GPC):
                            pick(loop, c)
                        show_picked(c)
                        loop.end()
                    split_low(i + 1)
                    add(i)

                rank_first()
                split_bias()
                step(0, 1)
                for c in range(1, CH + 1):
                    with dve.Fori(max(1, (c - 1) * GPC), min(c * GPC, G - 1)) as i:
                        step(i, c)
                group(G - 1)
                add(G - 1)

            @block.gpsimd
            def _(pool):
                pool.memset(b2_left[:, :], 0.0)
                pool.memset(mask16[:, :], 0.0).then_inc(zeroed, 1)
                pool.wait_ge(w_high, 1)
                pool.tensor_tensor(w1_l[:, :], w1s[:, :], w1_h[:, :].bitcast(F32), ALU.subtract).then_inc(w_low, 1)
                pool.wait_ge(t_high, 1)
                pool.tensor_tensor(t_l[:, :, :], t_in[:, :, :], t_h[:, :, :].bitcast(F32), ALU.subtract).then_inc(t_low, 1)
                pool.wait_ge(w_high, 2)
                pool.tensor_tensor(w2_l[:, :], w2s[:, :], w2_h[:, :].bitcast(F32), ALU.subtract).then_inc(w_low, 1)


_OUT = "out_dram"


def kernel(x, L0_tok_W, L0_tok_b, L0_attn_w_qkv, L0_attn_w_out, L0_attn_b_out, L0_ffn_w_gate_w, L0_ffn_w_gate_b,
           L0_ffn_W1, L0_ffn_b1, L0_ffn_W2, L0_ffn_b2):
    import numpy as np
    import concourse.bacc as bacc
    from concourse.bass_utils import run_bass_kernel_spmd

    def chunks(a):
        a = np.asarray(a)
        return a.reshape(-1, 128, a.shape[1]).transpose(1, 0, 2).reshape(128, -1)

    arrays = {
        "x": x, "w_patch": chunks(np.asarray(L0_tok_W).T), "b_patch": np.asarray(L0_tok_b).reshape(1, C),
        "w_qkv": chunks(L0_attn_w_qkv), "w_out": chunks(L0_attn_w_out), "b_out": np.asarray(L0_attn_b_out).reshape(1, C),
        "w_gate": chunks(L0_ffn_w_gate_w), "b_gate": np.asarray(L0_ffn_w_gate_b).reshape(1, E),
        "w1": chunks(np.asarray(L0_ffn_W1).transpose(1, 0, 2).reshape(C, E * SUB)),
        "b1": np.asarray(L0_ffn_b1).reshape(HID, 128).T,
        "w2": chunks(np.asarray(L0_ffn_W2).reshape(E * SUB, C)), "b2": np.asarray(L0_ffn_b2),
    }
    arrays.update(shape_constants(np))
    arrays = {name: np.ascontiguousarray(a) for name, a in arrays.items()}
    B = arrays["x"].shape[0]
    nc = bacc.Bacc("TRN2", target_bir_lowering=False, num_devices=1)
    args = [nc.dram_tensor(f"in_{name}", a.shape, mybir.dt.from_np(a.dtype), kind="ExternalInput").ap()
            for name, a in arrays.items()]
    args.append(nc.dram_tensor(_OUT, (B * SEQ, C), F32, kind="ExternalOutput").ap())
    vit_layer(nc, *args)
    r = run_bass_kernel_spmd(nc, [{f"in_{name}": a for name, a in arrays.items()}], core_ids=[0])
    return r.results[0][_OUT].reshape(B, SEQ, C)
```
